# Optimizing a Trainium2 kernel written in Bass

```python
import numpy as np
import jax
import jax.numpy as jnp

def _softmax(x, axis=-1):
    return jax.nn.softmax(x, axis=axis)

def _gelu(x):
    return jax.nn.gelu(x, approximate=True)

def _silu(x):
    return jax.nn.silu(x)

def _sigmoid(x):
    return jax.nn.sigmoid(x)

def _layernorm(x, axis=-1, eps=1e-05):
    m = jnp.mean(x, axis=axis, keepdims=True)
    v = jnp.var(x, axis=axis, keepdims=True)
    return (x - m) / jnp.sqrt(v + eps)

def _scatter_add(tgt, idx, src, axis=0):
    return tgt.at[idx].add(src)

def _segment_sum(src, seg, n):
    return jax.ops.segment_sum(src, seg, n)
kernel_name = 'mk_flamingo_gated_d2_seqx_r8_37bc33'

def setup_inputs(seed: int=0):
    np.random.seed(seed)
    _w = jnp.asarray

    def _rec_inputs():
        import jax
        import jax.numpy as jnp
        _rk = jax.random.key(seed)
        x = -0.0003929 + 0.9999 * jax.random.normal(jax.random.fold_in(_rk, 1), (2, 512, 128), jnp.float32)
        _lenS = 512 - jax.random.randint(jax.random.fold_in(_rk, 7), (2,), 0, max(1, 512 // 4) + 1, jnp.int32)
        _lenS2 = 154 - jax.random.randint(jax.random.fold_in(_rk, 8), (2,), 0, max(1, 154 // 4) + 1, jnp.int32)
        _ctx_768P = jax.random.normal(jax.random.fold_in(_rk, 11), (2, 16, 96), jnp.float32)
        _ctx_768c = jax.random.dirichlet(jax.random.fold_in(_rk, 511), 0.3 * jnp.ones((16,), jnp.float32), (2, 154))
        _ctx_768t = jnp.einsum('bsk,bkd->bsd', _ctx_768c, _ctx_768P)
        _ctx_768t = _ctx_768t * jax.lax.rsqrt(jnp.mean(jnp.square(_ctx_768t)) + 1e-12) * 0.953939
        ctx_768 = -0.00055796 + 0.999787 * (_ctx_768t + 0.3 * jax.random.normal(jax.random.fold_in(_rk, 611), (2, 154, 96), jnp.float32))
        _g = jax.random.normal(jax.random.fold_in(_rk, 9001), (2, 2), jnp.float32)
        _g = jnp.sign(_g) * jnp.maximum(jnp.abs(_g), 1.0) + (_g == 0) * 1.0
        g_xattn = _g[0]
        g_ffn = _g[1]
        return (x, ctx_768, g_xattn, g_ffn)
    x, ctx_768, g_xattn, g_ffn = _rec_inputs()

    def _L0_xattn_setup():
        import jax, jax.numpy as jnp
        import numpy as np
        IMAGE_DIM = 128
        TEXT_DIM = 96
        NUM_HEADS = 16
        HEAD_DIM = IMAGE_DIM // NUM_HEADS
        key = jax.random.key(seed)
        ks = jax.random.split(key, 14)
        B, N, M = (4, 512, 64)
        s_img = 1.0 / np.sqrt(IMAGE_DIM)
        s_txt = 1.0 / np.sqrt(TEXT_DIM)
        s_ff = 1.0 / np.sqrt(2 * IMAGE_DIM)
        return {'x': jax.random.normal(ks[0], (B, N, IMAGE_DIM), jnp.float32), 'y': jax.random.normal(ks[1], (B, M, TEXT_DIM), jnp.float32), 'Wq': jax.random.normal(ks[2], (IMAGE_DIM, IMAGE_DIM), jnp.float32) * s_img, 'bq': jax.random.normal(ks[3], (IMAGE_DIM,), jnp.float32) * s_img, 'Wk': jax.random.normal(ks[4], (TEXT_DIM, IMAGE_DIM), jnp.float32) * s_txt, 'bk': jax.random.normal(ks[5], (IMAGE_DIM,), jnp.float32) * s_txt, 'Wv': jax.random.normal(ks[6], (TEXT_DIM, IMAGE_DIM), jnp.float32) * s_txt, 'bv': jax.random.normal(ks[7], (IMAGE_DIM,), jnp.float32) * s_txt, 'W1': jax.random.normal(ks[8], (IMAGE_DIM, 2 * IMAGE_DIM), jnp.float32) * s_img, 'b1': jax.random.normal(ks[9], (2 * IMAGE_DIM,), jnp.float32) * s_img, 'W2': jax.random.normal(ks[10], (2 * IMAGE_DIM, IMAGE_DIM), jnp.float32) * s_ff, 'b2': jax.random.normal(ks[11], (IMAGE_DIM,), jnp.float32) * s_ff}
    _L0_xattn_all = _L0_xattn_setup()
    _L0_xattn_in = {k: v for k, v in _L0_xattn_all.items() if k in ('Wq', 'bq', 'Wk', 'bk', 'Wv', 'bv', 'W1', 'b1', 'W2', 'b2')}
    del _L0_xattn_all

    def _L0_ffn_setup():
        import jax, jax.numpy as jnp
        import numpy as np
        DIM = 128
        HIDDEN = 384
        SCALE = 1.0 / 127.0

        def _dequant(w_int, dtype):
            return w_int.astype(dtype) * jnp.asarray(SCALE, dtype)
        key = jax.random.key(seed)
        k_x, k_g, k_u, k_d = jax.random.split(key, 4)
        x = jax.random.normal(k_x, (4, 256, DIM), dtype=jnp.float32)
        w_gate = jax.random.randint(k_g, (HIDDEN, DIM), -127, 128, dtype=jnp.int32)
        w_up = jax.random.randint(k_u, (HIDDEN, DIM), -127, 128, dtype=jnp.int32)
        w_down = jax.random.randint(k_d, (DIM, HIDDEN), -127, 128, dtype=jnp.int32)
        return {'x': x, 'w_gate': w_gate, 'w_up': w_up, 'w_down': w_down}
    _L0_ffn_all = _L0_ffn_setup()
    _L0_ffn_in = {k: v for k, v in _L0_ffn_all.items() if k in ('w_gate', 'w_up', 'w_down')}
    del _L0_ffn_all

    def _L1_xattn_setup():
        import jax, jax.numpy as jnp
        import numpy as np
        NUM_HEADS = 16
        CLAMP = 10000.0
        key = jax.random.key(seed)
        ks = jax.random.split(key, 8)
        B, Nq, Nkv, Cq, Ckv = (4, 256, 256, 128, 96)
        s_q = 1.0 / np.sqrt(Cq)
        s_kv = 1.0 / np.sqrt(Ckv)
        return {'query': jax.random.normal(ks[0], (B, Nq, Cq), jnp.float32), 'key_value': jax.random.normal(ks[1], (B, Nkv, Ckv), jnp.float32), 'Wq': jax.random.normal(ks[2], (Cq, Cq), jnp.float32) * s_q, 'bq': jnp.zeros((Cq,), jnp.float32), 'Wk': jax.random.normal(ks[3], (Ckv, Cq), jnp.float32) * s_kv, 'bk': jnp.zeros((Cq,), jnp.float32), 'Wv': jax.random.normal(ks[4], (Ckv, Cq), jnp.float32) * s_kv, 'bv': jnp.zeros((Cq,), jnp.float32), 'Wo': jax.random.normal(ks[5], (Cq, Cq), jnp.float32) * s_q, 'bo': jnp.zeros((Cq,), jnp.float32)}
    _L1_xattn_all = _L1_xattn_setup()
    _L1_xattn_in = {k: v for k, v in _L1_xattn_all.items() if k in ('Wq', 'bq', 'Wk', 'bk', 'Wv', 'bv', 'Wo', 'bo')}
    del _L1_xattn_all

    def _L1_ffn_setup():
        import jax, jax.numpy as jnp
        import numpy as np
        D, F, E, K = (128, 344, 8, 2)
        key = jax.random.key(seed)
        k0, k1, k2, k3, k4 = jax.random.split(key, 5)
        s = 0.02
        x = jax.random.normal(k0, (2, 64, D), jnp.float32)
        Ws = jax.random.normal(k1, (D, E), jnp.float32) * s
        bs = jnp.zeros((E,), jnp.float32)
        Wg = jax.random.normal(k2, (E, D, F), jnp.float32) * s
        Wu = jax.random.normal(k3, (E, D, F), jnp.float32) * s
        Wd = jax.random.normal(k4, (E, F, D), jnp.float32) * s
        return {'x': x, 'Ws': Ws, 'bs': bs, 'Wg': Wg, 'Wu': Wu, 'Wd': Wd}
    _L1_ffn_all = _L1_ffn_setup()
    _L1_ffn_in = {k: v for k, v in _L1_ffn_all.items() if k in ('Ws', 'bs', 'Wg', 'Wu', 'Wd')}
    del _L1_ffn_all
    return {'x': x, 'ctx_768': ctx_768, 'g_xattn': g_xattn, 'g_ffn': g_ffn, 'L0_xattn_Wq': _L0_xattn_in['Wq'], 'L0_xattn_bq': _L0_xattn_in['bq'], 'L0_xattn_Wk': _L0_xattn_in['Wk'], 'L0_xattn_bk': _L0_xattn_in['bk'], 'L0_xattn_Wv': _L0_xattn_in['Wv'], 'L0_xattn_bv': _L0_xattn_in['bv'], 'L0_xattn_W1': _L0_xattn_in['W1'], 'L0_xattn_b1': _L0_xattn_in['b1'], 'L0_xattn_W2': _L0_xattn_in['W2'], 'L0_xattn_b2': _L0_xattn_in['b2'], 'L0_ffn_w_gate': _L0_ffn_in['w_gate'], 'L0_ffn_w_up': _L0_ffn_in['w_up'], 'L0_ffn_w_down': _L0_ffn_in['w_down'], 'L1_xattn_Wq': _L1_xattn_in['Wq'], 'L1_xattn_bq': _L1_xattn_in['bq'], 'L1_xattn_Wk': _L1_xattn_in['Wk'], 'L1_xattn_bk': _L1_xattn_in['bk'], 'L1_xattn_Wv': _L1_xattn_in['Wv'], 'L1_xattn_bv': _L1_xattn_in['bv'], 'L1_xattn_Wo': _L1_xattn_in['Wo'], 'L1_xattn_bo': _L1_xattn_in['bo'], 'L1_ffn_Ws': _L1_ffn_in['Ws'], 'L1_ffn_bs': _L1_ffn_in['bs'], 'L1_ffn_Wg': _L1_ffn_in['Wg'], 'L1_ffn_Wu': _L1_ffn_in['Wu'], 'L1_ffn_Wd': _L1_ffn_in['Wd']}

def reference(x, ctx_768, g_xattn, g_ffn, L0_xattn_Wq, L0_xattn_bq, L0_xattn_Wk, L0_xattn_bk, L0_xattn_Wv, L0_xattn_bv, L0_xattn_W1, L0_xattn_b1, L0_xattn_W2, L0_xattn_b2, L0_ffn_w_gate, L0_ffn_w_up, L0_ffn_w_down, L1_xattn_Wq, L1_xattn_bq, L1_xattn_Wk, L1_xattn_bk, L1_xattn_Wv, L1_xattn_bv, L1_xattn_Wo, L1_xattn_bo, L1_ffn_Ws, L1_ffn_bs, L1_ffn_Wg, L1_ffn_Wu, L1_ffn_Wd):
    import jax
    import jax.numpy as jnp

    def _L0_xattn_ref(x, y, Wq, bq, Wk, bk, Wv, bv, W1, b1, W2, b2):
        import jax, jax.numpy as jnp
        import numpy as np
        IMAGE_DIM = 128
        TEXT_DIM = 96
        NUM_HEADS = 16
        HEAD_DIM = IMAGE_DIM // NUM_HEADS
        B, N, _ = x.shape
        M = y.shape[1]
        q = (x @ Wq + bq).reshape(B, N, NUM_HEADS, HEAD_DIM)
        k = (y @ Wk + bk).reshape(B, M, NUM_HEADS, HEAD_DIM)
        v = (y @ Wv + bv).reshape(B, M, NUM_HEADS, HEAD_DIM)
        scale = 1.0 / np.sqrt(HEAD_DIM)
        scores = jnp.einsum('bnhd,bmhd->bhnm', q, k) * scale
        attn = jax.nn.softmax(scores, axis=-1)
        out = jnp.einsum('bhnm,bmhd->bnhd', attn, v).reshape(B, N, IMAGE_DIM)
        h = jax.nn.relu(out @ W1 + b1)
        return h @ W2 + b2

    def _L0_ffn_ref(x, w_gate, w_up, w_down):
        import jax, jax.numpy as jnp
        import numpy as np
        DIM = 128
        HIDDEN = 384
        SCALE = 1.0 / 127.0

        def _dequant(w_int, dtype):
            return w_int.astype(dtype) * jnp.asarray(SCALE, dtype)
        wg = _dequant(w_gate, x.dtype)
        wu = _dequant(w_up, x.dtype)
        wd = _dequant(w_down, x.dtype)
        gate = jnp.einsum('bsd,hd->bsh', x, wg)
        up = jnp.einsum('bsd,hd->bsh', x, wu)
        h = jax.nn.silu(gate) * up
        return jnp.einsum('bsh,dh->bsd', h, wd)

    def _L1_xattn_ref(query, key_value, Wq, bq, Wk, bk, Wv, bv, Wo, bo):
        import jax, jax.numpy as jnp
        import numpy as np
        NUM_HEADS = 16
        CLAMP = 10000.0
        B, Nq, Cq = query.shape
        Nkv = key_value.shape[1]
        H = NUM_HEADS
        D = Cq // H
        scale = D ** (-0.5)
        q = (query @ Wq + bq).reshape(B, Nq, H, D).transpose(0, 2, 1, 3)
        k = (key_value @ Wk + bk).reshape(B, Nkv, H, D).transpose(0, 2, 1, 3)
        v = (key_value @ Wv + bv).reshape(B, Nkv, H, D).transpose(0, 2, 1, 3)
        attn = jnp.einsum('bhqd,bhkd->bhqk', q, k) * scale
        attn = jnp.clip(attn, -CLAMP, CLAMP)
        attn = jax.nn.softmax(attn, axis=-1)
        attn = jnp.where(jnp.any(jnp.isnan(attn)), jnp.asarray(1.0 / Nkv, attn.dtype), attn)
        x = jnp.einsum('bhqk,bhkd->bqhd', attn, v).reshape(B, Nq, Cq)
        return x @ Wo + bo

    def _L1_ffn_ref(x, Ws, bs, Wg, Wu, Wd):
        import jax, jax.numpy as jnp
        import numpy as np
        D, F, E, K = (128, 344, 8, 2)
        b, n, d = x.shape
        xt = x.reshape(-1, d)
        logits = xt @ Ws + bs
        topk_w, topk_idx = jax.lax.top_k(logits, K)
        topk_w = jax.nn.softmax(topk_w, axis=-1)
        combine = jnp.sum(jax.nn.one_hot(topk_idx, E, dtype=xt.dtype) * topk_w[..., None], axis=1)
        g = jnp.einsum('td,edf->tef', xt, Wg)
        u = jnp.einsum('td,edf->tef', xt, Wu)
        h = jax.nn.silu(g) * u
        y = jnp.einsum('tef,efd->ted', h, Wd)
        out = jnp.einsum('ted,te->td', y, combine)
        return out.reshape(b, n, d)
    x = x + jnp.tanh(g_xattn[0]) * _L0_xattn_ref(_layernorm(x, axis=-1), ctx_768, L0_xattn_Wq, L0_xattn_bq, L0_xattn_Wk, L0_xattn_bk, L0_xattn_Wv, L0_xattn_bv, L0_xattn_W1, L0_xattn_b1, L0_xattn_W2, L0_xattn_b2)
    x = x + jnp.tanh(g_ffn[0]) * _L0_ffn_ref(_layernorm(x, axis=-1), L0_ffn_w_gate, L0_ffn_w_up, L0_ffn_w_down)
    x = x + jnp.tanh(g_xattn[1]) * _L1_xattn_ref(_layernorm(x, axis=-1), ctx_768, L1_xattn_Wq, L1_xattn_bq, L1_xattn_Wk, L1_xattn_bk, L1_xattn_Wv, L1_xattn_bv, L1_xattn_Wo, L1_xattn_bo)
    x = x + jnp.tanh(g_ffn[1]) * _L1_ffn_ref(_layernorm(x, axis=-1), L1_ffn_Ws, L1_ffn_bs, L1_ffn_Wg, L1_ffn_Wu, L1_ffn_Wd)
    return x

_drawn_inputs = setup_inputs


def setup_inputs(seed=0):
    import zlib

    import numpy as np

    out = dict(_drawn_inputs(seed))
    spreads = {'g_ffn': (-1.0, 0.6),
     'L1_xattn_bq': (0.0, 0.8),
     'L1_xattn_bk': (0.0, 2.0),
     'L1_xattn_bv': (0.0, 2.0),
     'L1_xattn_bo': (0.0, 2.0),
     'L1_ffn_bs': (0.0, 2.0)}
    factors = {'L0_xattn_bq': 3.776,
     'L0_xattn_bk': 64.0,
     'L1_xattn_Wq': 8.0,
     'L1_xattn_Wk': 8.0,
     'L1_xattn_Wv': 8.0,
     'L1_xattn_Wo': 8.0,
     'L1_ffn_Ws': 28.131,
     'L1_ffn_Wg': 27.734,
     'L1_ffn_Wu': 25.022,
     'L1_ffn_Wd': 24.939}
    for name, (base, spread) in spreads.items():
        noise = np.random.default_rng([zlib.crc32(name.encode()), seed]).standard_normal(out[name].shape)
        drawn = base * np.exp(spread * noise) if base else spread * noise
        out[name] = jnp.asarray(drawn.astype(out[name].dtype))
    for name, factor in factors.items():
        out[name] = (out[name] * factor).astype(out[name].dtype)
    return out
```

```python
import concourse.bass as bass
from concourse import mybir
from contextlib import ExitStack
import numpy as np

F32 = mybir.dt.float32
F32R = mybir.dt.float32r
I32 = mybir.dt.int32
U32 = mybir.dt.uint32
ALU = mybir.AluOpType
ACT = mybir.ActivationFunctionType
AX = mybir.AxisListType

B, T, D = 2, 512, 128
QT = T // 128
S, C = 154, 96
H, DH = 16, 8
G, J = 4, 4
SM = 128
SR = S - SM
KB = 160
HID = 2 * D
FH = 384
E, EF = 8, 344
FT = [128, 128, EF - 256]
SCALE = DH ** -0.5
CLAMP = 10000.0
FLOOR = 80.0
DEQ = 1.0 / 127.0
EPS = 1e-5

A_BANK, E_BANK, PV_BANK, TR_BANK, G_BANK = (0, 1), (2, 3), 4, 5, (6, 7)


def units():
    return [(l, b, j) for l in range(2) for b in range(B) for j in range(J)]


def schedule():
    at = [0, 1, 2, 3, 4, 5, 6, 7, 12, 13, 14, 15, 16, 17, 18, 19]
    unit_at = {s: u for u, s in enumerate(at)}
    chain = lambda b: [("join", 0, b), ("mlp_up", b, 0), ("mlp_up", b, 1), ("mlp_down", b), ("norm", 1, b),
                       ("turn", 1, b), ("ffn_up", b, 0), ("ffn_up", b, 1), ("ffn_up", b, 2), ("ffn_down", b),
                       ("norm", 2, b), ("turn", 2, b), ("query", 1, b)]
    last = lambda b: [("join", 1, b), ("out_proj", b), ("norm", 3, b), ("turn", 3, b), ("route", b)]
    between = {0: [("norm", 0, 1), ("turn", 0, 1), ("query", 0, 1)], 20: last(0), 24: last(1)}
    for first, steps in ((8, chain(0)), (12, chain(1))):
        for n, step in enumerate(steps):
            between.setdefault(first + n * 4 // len(steps), []).append(step)
    out = [("norm", 0, 0), ("turn", 0, 0), ("query", 0, 0)]
    for slot in range(25):
        scan, shift, exps, values, norm = (unit_at.get(slot - n) for n in range(5))
        fill = list(between.get(slot, []))
        for k in range(2 * QT):
            if scan is not None:
                out.append(("scan", scan, k))
            if k == 1 and shift is not None:
                out.append(("shift", shift))
            if k < 5 and exps is not None:
                out.append(("exps", exps, k))
            if k == 2 and values is not None:
                out.append(("values", values))
            if k == 5 and norm is not None:
                out.append(("share", norm))
            if k % 2 and fill:
                out.append(fill.pop(0))
        out += fill
    for b in range(B):
        out += [(kind, e, b) for e in range(E) for kind in ("expert_up", "expert_down")]
    return out


def turns(steps, users):
    out, n = {}, 0
    for step in steps:
        if step[0] in users:
            out[step] = n
            n += users[step[0]]
    return out


def flamingo(nc, a, out):
    STEPS = schedule()
    UNITS = units()
    SETUP = [("keys", 0), ("values_in", 0), ("values_in", 1), ("keys", 1)]
    g_turn = turns(SETUP + STEPS, {"keys": 1, "values_in": 1, "query": 1, "mlp_up": 1, "mlp_down": 1,
                                   "ffn_up": 2, "ffn_down": 1, "out_proj": 1, "route": 1})
    tr_turn = turns(STEPS, {"shift": 1, "share": 1, "join": 1, "turn": 1})
    join_no = turns(STEPS, {"join": 1})
    g_end = sum(g_turn[s] >= 0 for s in g_turn) + sum(s[0] == "ffn_up" for s in STEPS)

    ctx = ExitStack()
    with ctx:
        def sb(name, shape, dt=F32):
            return ctx.enter_context(nc.sbuf_tensor(name, shape, dt))

        def sem(name):
            return ctx.enter_context(nc.semaphore(name))

        x = sb("x", [128, B * QT, D])
        xn = sb("xn", [128, B, QT, D])
        xt = sb("xt", [128, B, T])
        x_hi = sb("x_hi", [128, B, T], F32R)
        x_lo = sb("x_lo", [128, B, T], F32R)
        qk_hi = sb("qk_hi", [128, B, T])
        qk_lo = sb("qk_lo", [128, B, T])
        q_st = [sb("q_st0", [128, B, J, T], F32R), sb("q_st1", [128, B, J, T], F32R)]
        k_st = [sb("k_st0", [128, J, B, G * KB], F32R), sb("k_st1", [128, J, B, G * KB], F32R)]
        v_main = sb("v_main", [128, 2, B, H, DH + 1])
        v_rest = sb("v_rest", [128, 2, B, J, 128])
        ex = sb("ex", [128, 2, 5, T])
        pv = sb("pv", [128, 2, T])
        o_tok = sb("o_tok", [128, B, QT, D])
        o_t = sb("o_t", [128, T])
        hid = sb("hid", [128, 3, T])
        sg = sb("sg", [128, T])
        ctx_t = sb("ctx_t", [C + 1, B, S])
        ctx_r = sb("ctx_r", [C + 1, B, G, 32])
        wk = sb("wk", [C + 1, 2, D])
        wv = sb("wv", [C + 1, 2, D])
        wq = sb("wq", [128, 2, D])
        bq = sb("bq", [128, 2])
        w1 = sb("w1", [128, HID])
        b1 = sb("b1", [128, 2])
        w2 = sb("w2", [128, 2, D])
        wo = sb("wo", [128, D])
        bias_out = sb("bias_out", [128, 2, D])
        f_w = sb("f_w", [128, 3, FH])
        ident = sb("ident", [128, 128])
        iota = sb("iota", [128, E])
        bs = sb("bs", [128, E])
        ws = sb("ws", [128, E])
        raw = sb("raw", [128, 4, EF])
        f_int = raw[:].rearrange("p n f -> p (n f)")[:, 0:3 * FH].bitcast(I32).rearrange("p (n f) -> p n f", n=3)
        eg_hi = sb("eg_hi", [128, E, EF], F32R)
        eu_hi = sb("eu_hi", [128, E, EF], F32R)
        eg_lo = k_st[0][:].rearrange("p j b c -> p (j b c)")[:, 0:E * EF].rearrange("p (e f) -> p e f", e=E)
        eu_lo = q_st[0][:].rearrange("p b j t -> p (b j t)")[:, 0:E * EF].rearrange("p (e f) -> p e f", e=E)
        ed = sb("ed", [128, E, 3, D])
        gate_in = sb("gate_in", [128, 4])
        gate = sb("gate", [128, 4])
        stats = sb("stats", [128, B, QT, 6])
        mv = sb("mv", [128, B, QT, 2])
        rstd = sb("rstd", [128, B, QT])
        mhalf = sb("mhalf", [128, QT])
        mx = sb("mx", [128, 2, QT, G])
        mx_parts = sb("mx_parts", [128, 2, QT, 2, G])
        m_rows = sb("m_rows", [2 * G, 2, T])
        rden = sb("rden", [128, QT, G])
        logit = sb("logit", [128, QT, E])
        top = sb("top", [128, QT, 8])
        top_i = sb("top_i", [128, QT, 8], U32)
        top_f = sb("top_f", [128, QT, 2])
        dl = sb("dl", [128, 3, QT])
        tw = sb("tw", [128, 2, QT])
        pick = sb("pick", [128, 2, QT, E])
        comb = sb("comb", [128, B, QT, E])
        ps = ctx.enter_context(nc.psum_tensor("ps", [128, 8, 512], F32))

        k_hi = [ex[:, l, 0, 0:B * S] for l in range(2)]
        k_lo = [ex[:, l, 1, 0:B * S] for l in range(2)]
        minus = ex[0:2, 0, 2:5, :].rearrange("p a t -> p (a t)")[:, 0:J * B * S]

        ld_ctx, ld_x, ld_q, ld_const, ld_vr = (sem(n) for n in ("ld_ctx", "ld_x", "ld_q", "ld_const", "ld_vr"))
        ld_mlp, ld_ffn, ld_moe, ld_gate = (sem(n) for n in ("ld_mlp", "ld_ffn", "ld_moe", "ld_gate"))
        ld_raw = [sem(f"ld_raw{n}") for n in range(4)]
        zeroed = sem("zeroed")
        zeroed1 = sem("zeroed1")
        ctx_ready = sem("ctx_ready")
        minus_ready = sem("minus_ready")
        k_hi_done = sem("k_hi_done")
        k_in = [sem(f"k_in{l}") for l in range(2)]
        minus_in = [sem(f"minus_in{l}") for l in range(2)]
        w_ready = sem("w_ready")
        tanh_done = sem("tanh_done")
        a_full, a_read = sem("a_full"), sem("a_read")
        e_full, e_read = sem("e_full"), sem("e_read")
        pv_full, pv_read = sem("pv_full"), sem("pv_read")
        tr_full, tr_read = sem("tr_full"), sem("tr_read")
        g_full = [sem("g_full0"), sem("g_full1")]
        g_read = [sem("g_read0"), sem("g_read1")]
        q_hi_done = sem("q_hi_done")
        q_in = [sem(f"q_in{n}") for n in range(2 * B)]
        max_split = sem("max_split")
        rows_in = [sem(f"rows_in{n}") for n in range(2)]
        clamped = sem("clamped")
        join_read = sem("join_read")
        var_done, rstd_done, xn_done = sem("var_done"), sem("rstd_done"), sem("xn_done")
        halves_hi, halves_done = sem("halves_hi"), sem("halves_done")
        biased = sem("biased")
        silu_done = sem("silu_done")
        gap_done, e_gap = sem("gap_done"), sem("e_gap")
        routed = sem("routed")
        chain = sem("chain")
        pool_chain = sem("pool_chain")
        split_done = sem("split_done")
        eg_full, eu_full, ed_full = sem("eg_full"), sem("eu_full"), sem("ed_full")
        e_silu, e_hid, e_added = sem("e_silu"), sem("e_hid"), sem("e_added")
        stored = sem("stored")

        def g_bank(turn):
            return ps[:, G_BANK[turn % 2], :]

        def wait_g_free(eng, turn):
            if turn >= 2:
                eng.wait_ge(g_read[turn % 2], turn // 2)

        def wait_g_full(eng, turn):
            eng.wait_ge(g_full[turn % 2], turn // 2 + 1)

        def wait_g_read(eng, turn):
            eng.wait_ge(g_read[turn % 2], turn // 2 + 1)

        tr = ps[:, TR_BANK, :]

        def KEY_PARTS(g):
            return ((slice(SM * g, SM * (g + 1)), slice(0, SM)),
                    (slice(SM * G + 32 * g, SM * G + 32 * g + SR), slice(SM, S)))

        K_MINUS, K_ALL = 16 * 2 * G, 16 * 2 * G * 3

        def uno(l, b, j):
            return (l * B + b) * J + j

        LAST = len(UNITS)

        block = ctx.enter_context(nc.Block())

        @block.sync
        def _(sp):
            sp.dma_start(ctx_t[0:C, :, :], a["ctx_t"]).then_inc(ld_ctx, 16)
            sp.dma_start(wk[:, :, :], a["wk"]).then_inc(ld_ctx, 16)
            sp.dma_start(wv[:, :, :], a["wv"]).then_inc(ld_ctx, 16)
            for b in range(B):
                sp.dma_start(x[:, b * QT:(b + 1) * QT, :], a["x"][b]).then_inc(ld_x, 16)
            sp.dma_start(v_rest[:].rearrange("p l b j c -> p (l b j) c"), a["v_rest0"]).then_inc(ld_vr, 16)
            for l in range(2):
                sp.wait_ge(minus_ready, 1)
                if l == 0:
                    sp.wait_ge(zeroed, 1)
                else:
                    sp.wait_ge(zeroed1, 1)
                for g in range(G):
                    for to, frm in KEY_PARTS(g):
                        sp.dma_start(k_st[l][32 * g + 24:32 * g + 26, :, :, to].bitcast(F32),
                                     minus.rearrange("p (j b s) -> p j b s", j=J, b=B)[:, :, :, frm])\
                            .then_inc(minus_in[l], 16)
                turn = g_turn[("keys", l)]
                wait_g_read(sp, turn)
                for g in range(G):
                    for r, src in enumerate((k_hi[l], k_hi[l], k_lo[l])):
                        for to, frm in KEY_PARTS(g):
                            sp.dma_start(k_st[l][32 * g + 8 * r:32 * g + 8 * r + 8, :, :, to].bitcast(F32),
                                         src[32 * g:32 * g + 32, :].rearrange("p (b s) -> p b s", b=B)[:, :, frm])\
                                .then_inc(k_in[l], 16)
                if l == 0:
                    sp.wait_ge(zeroed1, 1)
            for step in STEPS:
                if step[0] == "query":
                    _, l, b = step
                    wait_g_read(sp, g_turn[step])
                    for g in range(G):
                        for r, src in enumerate((qk_hi, qk_lo, qk_hi)):
                            sp.dma_start(q_st[l][32 * g + 8 * r:32 * g + 8 * r + 8, b, :, :].bitcast(F32),
                                         src[32 * g:32 * g + 32, b, :]).then_inc(q_in[l * B + b], 16)
                if step[0] == "shift":
                    u = step[1]
                    l, b, j = UNITS[u]
                    sp.wait_ge(tr_read, tr_turn[step] + 1)
                    for part in range(2):
                        first = 24 + part
                        sp.dma_start(q_st[l][first:first + 97:32, b, j, :].bitcast(F32),
                                     m_rows[G * part:G * part + G, u % 2, :]).then_inc(rows_in[u % 2], 16)
            for b in range(B):
                sp.wait_ge(e_added, E * (b + 1))
                sp.dma_start(out[b], x[:, b * QT:(b + 1) * QT, :]).then_inc(stored, 16)
            sp.wait_ge(stored, 16 * B)

        @block.gpsimd
        def _(pool):
            nc.gpsimd.memset(mhalf[:], -0.5)
            nc.gpsimd.memset(q_st[1][:].bitcast(U32), 0)
            nc.gpsimd.memset(k_st[1][:].bitcast(U32), 0).then_inc(zeroed1, 1)
            links = [0]

            def link(ins):
                links[0] += 1
                ins.then_inc(pool_chain, 1)
                pool.wait_ge(pool_chain, links[0])

            weights = [(w, e) for w in range(2) for e in range(E)]

            def load_raw(n):
                w, e = weights[n]
                nc.gpsimd.dma_start(raw[:, n % 4, :], a[("eg", "eu")[w]][e]).then_inc(ld_raw[n % 4], 16)

            def split(n):
                w, e = weights[n]
                hi, lo = (eg_hi, eu_hi)[w], (eg_lo, eu_lo)[w]
                pool.wait_ge(ld_raw[n % 4], 16 * (n // 4 + 1))
                link(nc.gpsimd.tensor_copy(hi[:, e, :], raw[:, n % 4, :]))
                nc.gpsimd.tensor_tensor(lo[:, e, :], raw[:, n % 4, :], hi[:, e, :].bitcast(F32),
                                        ALU.subtract).then_inc(split_done, 1)

            pool.wait_ge(zeroed1, 1)
            norms = splits = 0
            for step in STEPS:
                if step[0] == "norm":
                    _, i, b = step
                    norms += 1
                    pool.wait_ge(var_done, norms)
                    link(nc.gpsimd.tensor_scalar(rstd[:, b, :], mv[:, b, :, 1], EPS, None, ALU.add))
                    nc.gpsimd.tensor_tensor(rstd[:, b, :], rstd[:, b, :], mhalf[:], ALU.pow).then_inc(rstd_done, 1)
                    if i in (0, 2):
                        pool.wait_ge(xn_done, norms)
                        pool.wait_ge(w_ready, 1)
                        xb = x[:, b * QT:(b + 1) * QT, :]
                        nc.gpsimd.tensor_tensor(xb, xb, bias_out[:, i // 2:i // 2 + 1, :].broadcast_to([128, QT, D]),
                                                ALU.add).then_inc(biased, 1)
                if step[0] == "exps" and step[2] == 4 and step[1] >= B * J - 1 and splits < len(weights):
                    if splits == 0:
                        pool.wait_ge(e_full, 5 * B * J)
                        pool.wait_ge(w_ready, 2)
                        for n in range(4):
                            load_raw(n)
                    for n in range(splits, splits + 2):
                        split(n)
                    for n in range(splits + 4, min(splits + 6, len(weights))):
                        pool.wait_ge(split_done, n - 3)
                        load_raw(n)
                    splits += 2

        @block.scalar
        def _(act):
            act.dma_start(ident[:], a["ident"]).then_inc(ld_const, 16)
            act.dma_start(wq[:], a["wq"]).then_inc(ld_q, 16)
            act.dma_start(bq[:], a["bq"]).then_inc(ld_q, 16)
            act.dma_start(gate_in[:], a["gates"]).then_inc(ld_gate, 16)
            act.dma_start(bias_out[:], a["bias_out"]).then_inc(ld_gate, 16)
            act.dma_start(w1[:], a["w1"]).then_inc(ld_mlp, 16)
            act.dma_start(b1[:], a["b1"]).then_inc(ld_mlp, 16)
            act.dma_start(w2[:], a["w2"]).then_inc(ld_mlp, 16)
            act.dma_start(f_int, a["f_int"]).then_inc(ld_ffn, 16)
            act.dma_start(wo[:], a["wo"]).then_inc(ld_moe, 16)
            act.dma_start(iota[:], a["iota"]).then_inc(ld_moe, 16)
            act.dma_start(bs[:], a["bs"]).then_inc(ld_moe, 16)
            act.dma_start(ws[:], a["ws"]).then_inc(ld_moe, 16)
            act.dma_start(ed[:, :, 0:2, :].rearrange("p e t d -> p e (t d)"), a["ed01"]).then_inc(ld_moe, 16)
            act.dma_start(ed[0:FT[2], :, 2, :], a["ed2"]).then_inc(ld_moe, 16)
            act.wait_ge(ld_gate, 32)
            nc.scalar.activation(gate[:], gate_in[:], ACT.Tanh).then_inc(tanh_done, 1)
            for step in SETUP:
                if step[0] == "keys":
                    l = step[1]
                    turn = g_turn[step]
                    wait_g_full(act, turn)
                    nc.scalar.activation(k_hi[l].bitcast(F32R), g_bank(turn)[:, 0:B * S], ACT.Copy)\
                        .then_inc(k_hi_done, 1)
            ups = 0
            for step in STEPS:
                kind = step[0]
                if kind == "query":
                    _, l, b = step
                    turn = g_turn[step]
                    wait_g_full(act, turn)
                    if l:
                        act.wait_ge(q_in[b], 16 * 3 * G)
                    act.wait_ge(w_ready, 1)
                    nc.scalar.activation(qk_hi[:, b, :].bitcast(F32R), g_bank(turn), ACT.Identity,
                                         bias=bq[:, l:l + 1]).then_inc(q_hi_done, 1)
                elif kind == "shift":
                    u = step[1]
                    act.wait_ge(tr_full, tr_turn[step] + 1)
                    if u >= 2:
                        act.wait_ge(rows_in[u % 2], 32 * (u // 2))
                    nc.scalar.copy(m_rows[:, u % 2, :], tr[0:2 * G, :]).then_inc(tr_read, 1)
                elif kind == "exps":
                    _, u, t = step
                    n = 5 * u + t
                    if t == 0 and u < 2:
                        act.wait_ge(k_in[u], K_ALL)
                        if u == 0:
                            act.wait_ge(minus_in[0], K_MINUS)
                            act.wait_ge(minus_in[1], K_MINUS)
                    if t == 0 and u >= 2:
                        act.wait_ge(pv_full, u - 1)
                    act.wait_ge(e_full, n + 1)
                    nc.scalar.activation(ex[:, u % 2, t, :], ps[:, E_BANK[n % 2], :], ACT.Exp).then_inc(e_read, 1)
                elif kind == "values":
                    u = step[1]
                    act.wait_ge(pv_full, u + 1)
                    if u >= 2:
                        act.wait_ge(tr_full, tr_turn[("share", u - 2)] + 1)
                    nc.scalar.copy(pv[:, u % 2, :], ps[:, PV_BANK, :]).then_inc(pv_read, 1)
                elif kind == "join":
                    n = join_no[step]
                    act.wait_ge(tr_full, tr_turn[step] + 1)
                    if n >= 1:
                        before = [s for s in STEPS if s[0] == "join"][n - 1]
                        if before[1] == 0:
                            wait_g_full(act, g_turn[("mlp_up", before[2], 1)])
                        else:
                            wait_g_full(act, g_turn[("out_proj", before[2])])
                    nc.scalar.copy(o_t[:], tr).then_inc(tr_read, 1)
                elif kind == "turn":
                    _, i, b = step
                    act.wait_ge(tr_full, tr_turn[step] + 1)
                    nc.scalar.copy(xt[:, b, :], tr).then_inc(tr_read, 1)
                    if i == 3:
                        act.wait_ge(tr_read, tr_turn[step] + 1)
                        nc.scalar.copy(x_hi[:, b, :], xt[:, b, :]).then_inc(halves_hi, 1)
                elif kind == "mlp_up":
                    _, b, f = step
                    turn = g_turn[step]
                    wait_g_full(act, turn)
                    if b:
                        wait_g_full(act, g_turn[("ffn_down", b - 1)])
                    nc.scalar.activation(hid[:, f, :], g_bank(turn), ACT.Relu, bias=b1[:, f:f + 1])\
                        .then_inc(g_read[turn % 2], 1)
                elif kind == "ffn_up":
                    _, b, f = step
                    turn = g_turn[step]
                    wait_g_full(act, turn)
                    if ups:
                        wait_g_read(act, last_up + 1)
                    nc.scalar.activation(sg[:], g_bank(turn), ACT.Silu).then_inc(g_read[turn % 2], 1)
                    last_up = turn
                    ups += 1
                elif kind == "route":
                    b = step[1]
                    act.wait_ge(gap_done, b + 1)
                    nc.scalar.activation(dl[:, 1, :], dl[:, 0, :], ACT.Exp).then_inc(e_gap, 1)
                elif kind == "expert_up":
                    _, e, b = step
                    for f, rows in enumerate(FT):
                        n = (b * E + e) * 3 + f
                        act.wait_ge(eg_full, n + 1)
                        if n >= 2:
                            act.wait_ge(e_hid, n - 1)
                        else:
                            act.wait_ge(pv_full, LAST)
                        nc.scalar.activation(ex[0:rows, n % 2, 3, :], ps[0:rows, (0, 1)[n % 2], :], ACT.Silu)\
                            .then_inc(e_silu, 1)

        @block.vector
        def _(dve):
            links = [0]

            def link(ins):
                links[0] += 1
                ins.then_inc(chain, 1)
                dve.wait_ge(chain, links[0])

            nc.vector.memset(minus, -1.0).then_inc(minus_ready, 1)
            link(nc.vector.memset(ctx_r[:], 0.0))
            dve.wait_ge(ld_ctx, 48)
            nc.vector.memset(ctx_t[C:C + 1, :, :], 1.0).then_inc(chain, 1)
            links[0] += 1
            dve.wait_ge(chain, links[0])
            for b in range(B):
                last = nc.vector.tensor_copy(ctx_r[:, b, :, 0:SR],
                                             ctx_t[:, b, SM:S].unsqueeze(1).broadcast_to([C + 1, G, SR]))
            last.then_inc(ctx_ready, 1)
            nc.vector.memset(k_st[0][:].bitcast(U32), 0).then_inc(zeroed, 1)
            nc.vector.memset(q_st[0][:].bitcast(U32), 0)
            nc.vector.memset(v_main[:], 1.0).then_inc(zeroed, 1)
            dve.wait_ge(ld_q, 32)
            nc.vector.tensor_scalar(wq[:], wq[:], SCALE, None, ALU.mult)
            nc.vector.tensor_scalar(bq[:], bq[:], SCALE, None, ALU.mult)
            dve.wait_ge(tanh_done, 1)
            for l in range(2):
                last = nc.vector.tensor_scalar(bias_out[:, l, :], bias_out[:, l, :], gate[:, l:l + 1], None, ALU.mult)
            last.then_inc(w_ready, 1)
            for step in SETUP:
                turn = g_turn[step]
                wait_g_full(dve, turn)
                if step[0] == "keys":
                    l = step[1]
                    dve.wait_ge(k_hi_done, l + 1)
                    nc.vector.tensor_tensor(k_lo[l].bitcast(F32R), g_bank(turn)[:, 0:B * S], k_hi[l],
                                            ALU.subtract).then_inc(g_read[turn % 2], 1)
                else:
                    b = step[1]
                    if b == 0:
                        dve.wait_ge(ld_vr, 16)
                        dve.wait_ge(zeroed, 2)
                    bank = g_bank(turn)
                    nc.vector.tensor_copy(v_main[:, :, b, :, 0:DH],
                                          bank[:, 0:2 * D].rearrange("p (l h d) -> p l h d", l=2, h=H))
                    for g in range(G):
                        for l in range(2):
                            rows = slice(32 * g, 32 * g + 32)
                            first = 2 * D + l * D + 32 * g
                            last = nc.vector.tensor_copy(
                                v_rest[rows, l, b, :, 32 * g:32 * g + DH],
                                bank[rows, first:first + 32].rearrange("p (j d) -> p j d", j=J))
                    last.then_inc(g_read[turn % 2], 1)
            dve.wait_ge(ld_ffn, 16)
            nc.vector.tensor_scalar(f_w[:], f_int, DEQ, None, ALU.mult).then_inc(w_ready, 1)
            norms = silus = scans = 0
            for step in STEPS:
                kind = step[0]
                if kind == "norm":
                    _, i, b = step
                    norms += 1
                    if i == 0:
                        dve.wait_ge(ld_x, 16 * B)
                    elif i in (1, 3):
                        wait_g_read(dve, g_turn[("mlp_down", b) if i == 1 else ("out_proj", b)])
                    else:
                        wait_g_read(dve, g_turn[("ffn_down", b)])
                    for q in range(QT):
                        last = nc.vector.bn_stats(stats[:, b, q, :], x[:, b * QT + q, :])
                    link(last)
                    for q in range(QT):
                        last = nc.vector.bn_aggr(mv[:, b, q, :], stats[:, b, q, :])
                    last.then_inc(var_done, 1)
                    dve.wait_ge(rstd_done, norms)
                    dve.wait_ge(var_done, norms)
                    if i:
                        dve.wait_ge(tr_full, tr_turn[("turn", i - 1, b)] + 1)
                    for q in range(QT):
                        last = nc.vector.tensor_scalar(xn[:, b, q, :], x[:, b * QT + q, :], mv[:, b, q, 0:1],
                                                       rstd[:, b, q:q + 1], ALU.subtract, ALU.mult)
                    last.then_inc(xn_done, 1)
                elif kind == "turn":
                    _, i, b = step
                    if i == 3:
                        dve.wait_ge(halves_hi, b + 1)
                        nc.vector.tensor_tensor(x_lo[:, b, :], xt[:, b, :], x_hi[:, b, :].bitcast(F32),
                                                ALU.subtract).then_inc(halves_done, 1)
                elif kind == "query":
                    _, l, b = step
                    turn = g_turn[step]
                    dve.wait_ge(q_hi_done, l * B + b + 1)
                    nc.vector.scalar_tensor_tensor(qk_lo[:, b, :].bitcast(F32R), g_bank(turn), bq[:, l:l + 1],
                                                   qk_hi[:, b, :], ALU.add, ALU.subtract)\
                        .then_inc(g_read[turn % 2], 1)
                elif kind == "scan":
                    _, u, k = step
                    n = 2 * QT * u + k
                    dve.wait_ge(a_full, n + 1)
                    nc.vector.tensor_reduce(mx[:, u % 2, k // 2, 2 * (k % 2):2 * (k % 2) + 2],
                                            ps[:, A_BANK[n % 2], 0:2 * S].rearrange("p (h s) -> p h s", h=2),
                                            AX.X, ALU.max).then_inc(a_read, 1)
                elif kind == "shift":
                    u = step[1]
                    dve.wait_ge(a_read, 2 * QT * (u + 1))
                    m = mx[:, u % 2, :, :]
                    if UNITS[u][0] == 1:
                        link(nc.vector.tensor_scalar(m, m, FLOOR - CLAMP, CLAMP, ALU.max, ALU.min))
                    if u >= 2:
                        dve.wait_ge(tr_full, tr_turn[("shift", u - 2)] + 1)
                    link(nc.vector.tensor_copy(mx_parts[:, u % 2, :, 0, :].bitcast(F32R), m))
                    nc.vector.tensor_tensor(mx_parts[:, u % 2, :, 1, :].bitcast(F32R), m,
                                            mx_parts[:, u % 2, :, 0, :], ALU.subtract).then_inc(max_split, 1)
                elif kind == "values":
                    u = step[1]
                    if UNITS[u][0] == 1:
                        dve.wait_ge(e_read, 5 * (u + 1))
                        w = ex[:, u % 2, :, :]
                        nc.vector.tensor_scalar(w, w, float(np.exp(-FLOOR)), 1.0, ALU.max, ALU.min)\
                            .then_inc(clamped, 1)
                elif kind == "share":
                    u = step[1]
                    l, b, j = UNITS[u]
                    dve.wait_ge(tr_full, tr_turn[step] + 1)
                    t4 = tr.rearrange("p (q g c) -> p q g c", q=QT, g=G)
                    link(nc.vector.reciprocal(rden[:], t4[:, :, :, DH]))
                    if l and j == 0:
                        dve.wait_ge(tr_full, tr_turn[("join", 0, b)] + 1)
                    nc.vector.tensor_tensor(
                        o_tok[:, b, :, :].rearrange("p q (g j d) -> p q g j d", g=G, j=J)[:, :, :, j, :],
                        t4[:, :, :, 0:DH], rden[:].unsqueeze(3).broadcast_to([128, QT, G, DH]),
                        ALU.mult).then_inc(tr_read, 1)
                elif kind in ("mlp_down", "out_proj", "ffn_down"):
                    b = step[1]
                    turn = g_turn[step]
                    wait_g_full(dve, turn)
                    col = {"mlp_down": 0, "out_proj": 1, "ffn_down": 2}[kind]
                    if kind != "ffn_down":
                        norm_before = [s for s in STEPS if s[0] == "norm" and s[1] in (0, 2)]
                        dve.wait_ge(biased, norm_before.index(("norm", 2 * col, b)) + 1)
                    xb = x[:, b * QT:(b + 1) * QT, :].rearrange("p q d -> p (q d)")
                    nc.vector.scalar_tensor_tensor(xb, g_bank(turn), gate[:, col:col + 1], xb, ALU.mult, ALU.add)\
                        .then_inc(g_read[turn % 2], 1)
                elif kind == "ffn_up":
                    _, b, f = step
                    turn = g_turn[step]
                    wait_g_read(dve, turn)
                    wait_g_full(dve, turn + 1)
                    nc.vector.tensor_tensor(hid[:, f, :], sg[:], g_bank(turn + 1), ALU.mult)\
                        .then_inc(g_read[(turn + 1) % 2], 1)
                elif kind == "route":
                    b = step[1]
                    turn = g_turn[step]
                    if b == 0:
                        dve.wait_ge(ld_moe, 16 * 6)
                    wait_g_full(dve, turn)
                    bank = g_bank(turn)[:, 0:QT * E].rearrange("p (q e) -> p q e", q=QT)
                    nc.vector.tensor_tensor(logit[:], bank, bs[:].unsqueeze(1).broadcast_to([128, QT, E]),
                                            ALU.add).then_inc(g_read[turn % 2], 1)
                    wait_g_read(dve, turn)
                    for q in range(QT):
                        last = nc.vector.max(top[:, q, :], logit[:, q, :])
                    link(last)
                    for q in range(QT):
                        last = nc.vector.max_index(top_i[:, q, :], top[:, q, :], logit[:, q, :])
                    link(last)
                    nc.vector.tensor_tensor(dl[:, 0, :], top[:, :, 1], top[:, :, 0], ALU.subtract)\
                        .then_inc(gap_done, 1)
                    link(nc.vector.tensor_copy(top_f[:], top_i[:, :, 0:2]))
                    dve.wait_ge(e_gap, b + 1)
                    link(nc.vector.tensor_scalar(dl[:, 2, :], dl[:, 1, :], 1.0, None, ALU.add))
                    link(nc.vector.reciprocal(tw[:, 0, :], dl[:, 2, :]))
                    link(nc.vector.tensor_scalar(tw[:, 0, :], tw[:, 0, :], gate[:, 3:4], None, ALU.mult))
                    link(nc.vector.tensor_tensor(tw[:, 1, :], tw[:, 0, :], dl[:, 1, :], ALU.mult))
                    for n in range(2):
                        link(nc.vector.tensor_tensor(pick[:, n, :, :], iota[:].unsqueeze(1).broadcast_to([128, QT, E]),
                                                     top_f[:, :, n:n + 1].broadcast_to([128, QT, E]), ALU.is_equal))
                        link(nc.vector.tensor_tensor(pick[:, n, :, :], pick[:, n, :, :],
                                                     tw[:, n, :].unsqueeze(2).broadcast_to([128, QT, E]), ALU.mult))
                    nc.vector.tensor_tensor(comb[:, b, :, :], pick[:, 0, :, :], pick[:, 1, :, :], ALU.add)\
                        .then_inc(routed, 1)
                elif kind == "expert_up":
                    _, e, b = step
                    for f, rows in enumerate(FT):
                        n = (b * E + e) * 3 + f
                        dve.wait_ge(e_silu, n + 1)
                        dve.wait_ge(eu_full, n + 1)
                        if f == 0 and n >= 6:
                            dve.wait_ge(ed_full, b * E + e - 1)
                        nc.vector.tensor_tensor(ex[0:rows, (b * E + e) % 2, f, :], ex[0:rows, n % 2, 3, :],
                                                ps[0:rows, (2, 3)[n % 2], :], ALU.mult).then_inc(e_hid, 1)
                elif kind == "expert_down":
                    _, e, b = step
                    n = b * E + e
                    dve.wait_ge(ed_full, n + 1)
                    dve.wait_ge(routed, b + 1)
                    if e:
                        dve.wait_ge(e_added, n)
                    for q in range(QT):
                        xb = x[:, b * QT + q, :]
                        last = nc.vector.scalar_tensor_tensor(xb, ps[:, (4, 5)[n % 2], q * D:(q + 1) * D],
                                                              comb[:, b, q, e:e + 1], xb, ALU.mult, ALU.add)
                    last.then_inc(e_added, 1)

        @block.tensor
        def _(pe):
            def mm(o, lhsT, rhs, start=True, stop=True):
                return nc.tensor.matmul(o, lhsT, rhs, start=start, stop=stop, skip_group_check=True)

            pe.wait_ge(ctx_ready, 1)
            for step in SETUP:
                turn = g_turn[step]
                wait_g_free(pe, turn)
                bank = g_bank(turn)
                if step[0] == "keys":
                    last = mm(bank[:, 0:B * S], wk[:, step[1], :], ctx_t[:].rearrange("c b s -> c (b s)"))
                else:
                    b = step[1]
                    mm(bank[:, 0:2 * D], ctx_t[:, b, 0:SM], wv[:].rearrange("c l d -> c (l d)"))
                    last = mm(bank[:, 2 * D:4 * D], ctx_r[:, b, :, :].rearrange("c g k -> c (g k)"),
                              wv[:].rearrange("c l d -> c (l d)"))
                last.then_inc(g_full[turn % 2], 1)
            pe.wait_ge(ld_const, 16)
            norms = 0
            for step in STEPS:
                kind = step[0]
                if kind == "norm":
                    norms += 1
                elif kind == "turn":
                    _, i, b = step
                    turn = tr_turn[step]
                    pe.wait_ge(xn_done, norms)
                    if turn:
                        pe.wait_ge(tr_read, turn)
                    for q in range(QT):
                        last = nc.tensor.transpose(tr[:, q * 128:(q + 1) * 128], xn[:, b, q, :], ident[:])
                    last.then_inc(tr_full, 1)
                elif kind == "query":
                    _, l, b = step
                    turn = g_turn[step]
                    wait_g_free(pe, turn)
                    pe.wait_ge(w_ready, 1)
                    pe.wait_ge(tr_read, tr_turn[("turn", 2 * l, b)] + 1)
                    mm(g_bank(turn), wq[:, l, :], xt[:, b, :]).then_inc(g_full[turn % 2], 1)
                elif kind == "scan":
                    _, u, k = step
                    l, b, j = UNITS[u]
                    n = 2 * QT * u + k
                    if k == 0 and j == 0:
                        pe.wait_ge(q_in[l * B + b], 16 * 3 * G)
                        pe.wait_ge(k_in[l], K_ALL)
                        pe.wait_ge(minus_in[l], K_MINUS)
                    if n >= 2:
                        pe.wait_ge(a_read, n - 1)
                    half = k % 2
                    queries = q_st[l][:, b, j, (k // 2) * 128:(k // 2 + 1) * 128]
                    o = ps[:, A_BANK[n % 2], 0:2 * S].rearrange("p (h s) -> p h s", h=2)
                    rest = k_st[l][:, j, b, SM * G + 64 * half:SM * G + 64 * (half + 1)]
                    mm(o[:, :, 0:SM], queries, k_st[l][:, j, b, 2 * SM * half:2 * SM * (half + 1)])
                    mm(o[:, :, SM:S], queries, rest.rearrange("p (h s) -> p h s", h=2)[:, :, 0:SR])\
                        .then_inc(a_full, 1)
                elif kind == "shift":
                    u = step[1]
                    turn = tr_turn[step]
                    pe.wait_ge(max_split, u + 1)
                    if turn:
                        pe.wait_ge(tr_read, turn)
                    for q in range(QT):
                        last = nc.tensor.transpose(tr[0:2 * G, q * 128:(q + 1) * 128],
                                                   mx_parts[:, u % 2, q, :, :].rearrange("p a g -> p (a g)"), ident[:])
                    last.then_inc(tr_full, 1)
                elif kind == "exps":
                    _, u, t = step
                    l, b, j = UNITS[u]
                    n = 5 * u + t
                    if t == 0:
                        pe.wait_ge(rows_in[u % 2], 32 * (u // 2 + 1))
                    if n >= 2:
                        pe.wait_ge(e_read, n - 1)
                    first = SM * G if t == 0 else SM * (t - 1)
                    keys = k_st[l][:, j, b, first:first + SM]
                    mm(ps[:, E_BANK[n % 2], :], keys, q_st[l][:, b, j, :]).then_inc(e_full, 1)
                elif kind == "values":
                    u = step[1]
                    l, b, j = UNITS[u]
                    if l:
                        pe.wait_ge(clamped, u - B * J + 1)
                    else:
                        pe.wait_ge(e_read, 5 * (u + 1))
                    if u:
                        pe.wait_ge(pv_read, u)
                    mm(ps[:, PV_BANK, :], v_rest[:, l, b, j, :], ex[:, u % 2, 0, :], stop=False)
                    for g in range(G):
                        last = mm(ps[32 * g:32 * g + DH + 1, PV_BANK, :], v_main[:, l, b, J * g + j, :],
                                  ex[:, u % 2, 1 + g, :], start=False)
                    last.then_inc(pv_full, 1)
                elif kind == "share":
                    u = step[1]
                    turn = tr_turn[step]
                    pe.wait_ge(pv_read, u + 1)
                    pe.wait_ge(tr_read, turn)
                    for q in range(QT):
                        last = nc.tensor.transpose(tr[:, q * 128:(q + 1) * 128], pv[:, u % 2, q * 128:(q + 1) * 128],
                                                   ident[:])
                    last.then_inc(tr_full, 1)
                elif kind == "join":
                    _, l, b = step
                    turn = tr_turn[step]
                    pe.wait_ge(tr_read, turn)
                    for q in range(QT):
                        last = nc.tensor.transpose(tr[:, q * 128:(q + 1) * 128], o_tok[:, b, q, :], ident[:])
                    last.then_inc(tr_full, 1)
                elif kind == "mlp_up":
                    _, b, f = step
                    turn = g_turn[step]
                    if f == 0:
                        pe.wait_ge(ld_mlp, 48)
                        pe.wait_ge(tr_read, tr_turn[("join", 0, b)] + 1)
                    wait_g_free(pe, turn)
                    mm(g_bank(turn), w1[:, f * 128:(f + 1) * 128], o_t[:]).then_inc(g_full[turn % 2], 1)
                elif kind == "mlp_down":
                    b = step[1]
                    turn = g_turn[step]
                    for f in range(2):
                        wait_g_read(pe, g_turn[("mlp_up", b, f)])
                    wait_g_free(pe, turn)
                    for q in range(QT):
                        for f in range(2):
                            last = mm(g_bank(turn)[:, q * D:(q + 1) * D], hid[:, f, q * 128:(q + 1) * 128],
                                      w2[:, f, :], start=(f == 0), stop=(f == 1))
                    last.then_inc(g_full[turn % 2], 1)
                elif kind == "out_proj":
                    b = step[1]
                    turn = g_turn[step]
                    pe.wait_ge(ld_moe, 16 * 6)
                    pe.wait_ge(tr_read, tr_turn[("join", 1, b)] + 1)
                    wait_g_free(pe, turn)
                    for q in range(QT):
                        last = mm(g_bank(turn)[:, q * D:(q + 1) * D], o_t[:, q * 128:(q + 1) * 128], wo[:])
                    last.then_inc(g_full[turn % 2], 1)
                elif kind == "ffn_up":
                    _, b, f = step
                    turn = g_turn[step]
                    if f == 0:
                        pe.wait_ge(w_ready, 2)
                        pe.wait_ge(tr_read, tr_turn[("turn", 1, b)] + 1)
                    for n in range(2):
                        wait_g_free(pe, turn + n)
                        mm(g_bank(turn + n), f_w[:, n, f * 128:(f + 1) * 128], xt[:, b, :])\
                            .then_inc(g_full[(turn + n) % 2], 1)
                elif kind == "ffn_down":
                    b = step[1]
                    turn = g_turn[step]
                    for f in range(3):
                        wait_g_read(pe, g_turn[("ffn_up", b, f)] + 1)
                    wait_g_free(pe, turn)
                    for q in range(QT):
                        for f in range(3):
                            last = mm(g_bank(turn)[:, q * D:(q + 1) * D], hid[:, f, q * 128:(q + 1) * 128],
                                      f_w[:, 2, f * 128:(f + 1) * 128], start=(f == 0), stop=(f == 2))
                    last.then_inc(g_full[turn % 2], 1)
                elif kind == "route":
                    b = step[1]
                    turn = g_turn[step]
                    pe.wait_ge(tr_read, tr_turn[("turn", 3, b)] + 1)
                    wait_g_free(pe, turn)
                    for q in range(QT):
                        last = mm(g_bank(turn)[:, q * E:(q + 1) * E], xt[:, b, q * 128:(q + 1) * 128], ws[:])
                    last.then_inc(g_full[turn % 2], 1)
                elif kind == "expert_up":
                    _, e, b = step
                    if e == 0:
                        pe.wait_ge(halves_done, b + 1)
                        pe.wait_ge(split_done, 2 * E)
                        if b == 0:
                            pe.wait_ge(a_read, 2 * QT * LAST)
                            pe.wait_ge(e_read, 5 * LAST)
                            pe.wait_ge(pv_read, LAST)
                            pe.wait_ge(tr_read, len(tr_turn))
                    for f, rows in enumerate(FT):
                        n = (b * E + e) * 3 + f
                        cols = slice(f * 128, f * 128 + rows)
                        for hi, lo, bank, full, used in ((eg_hi, eg_lo, (0, 1), eg_full, e_silu),
                                                         (eu_hi, eu_lo, (2, 3), eu_full, e_hid)):
                            if n >= 2:
                                pe.wait_ge(used, n - 1)
                            o = ps[0:rows, bank[n % 2], :]
                            mm(o, hi[:, e, cols], x_hi[:, b, :], stop=False)
                            mm(o, hi[:, e, cols], x_lo[:, b, :], start=False, stop=False)
                            mm(o, lo[:, e, cols], x_hi[:, b, :], start=False).then_inc(full, 1)
                elif kind == "expert_down":
                    _, e, b = step
                    n = b * E + e
                    pe.wait_ge(e_hid, 3 * (n + 1))
                    if n >= 2:
                        pe.wait_ge(e_added, n - 1)
                    for q in range(QT):
                        for f, rows in enumerate(FT):
                            last = mm(ps[:, (4, 5)[n % 2], q * D:(q + 1) * D],
                                      ex[0:rows, n % 2, f, q * 128:(q + 1) * 128], ed[0:rows, e, f, :],
                                      start=(f == 0), stop=(f == 2))
                    last.then_inc(ed_full, 1)


def kernel(**inputs):
    import numpy as _np
    import concourse.bacc as _bacc
    from concourse import mybir as _mybir
    from concourse.bass_utils import run_bass_kernel_spmd as _run

    i = {k: _np.asarray(v) for k, v in inputs.items()}
    tok = lambda v: v.reshape(B, QT, 128, D).transpose(0, 2, 1, 3)
    heads = lambda v: v.reshape(-1, G, J, DH).transpose(0, 1, 3, 2).reshape(-1, D)
    row = lambda v, n=128: _np.broadcast_to(v.reshape(1, -1), (n, v.size))
    ctx_rows = lambda w, b: _np.concatenate([w, b.reshape(1, -1)], 0)
    v_rest0 = _np.zeros((128, 128), _np.float32)
    for g in range(G):
        v_rest0[32 * g:32 * g + SR, 32 * g + DH] = 1.0
    down = i["L1_ffn_Wd"]
    arrays = {
        "x": tok(i["x"]),
        "ctx_t": i["ctx_768"].transpose(2, 0, 1),
        "wk": _np.stack([ctx_rows(heads(i[f"L{l}_xattn_Wk"]), heads(i[f"L{l}_xattn_bk"])) for l in range(2)], 1),
        "wv": _np.stack([ctx_rows(i[f"L{l}_xattn_Wv"], i[f"L{l}_xattn_bv"]) for l in range(2)], 1),
        "wq": _np.stack([heads(i[f"L{l}_xattn_Wq"]) for l in range(2)], 1),
        "bq": _np.stack([heads(i[f"L{l}_xattn_bq"])[0] for l in range(2)], 1),
        "v_rest0": _np.broadcast_to(v_rest0[:, None, :], (128, 2 * B * J, 128)),
        "ident": _np.eye(128, dtype=_np.float32),
        "iota": row(_np.arange(E, dtype=_np.float32)),
        "gates": row(_np.concatenate([i["g_xattn"], i["g_ffn"]])),
        "bias_out": _np.broadcast_to(_np.stack([i["L0_xattn_b2"], i["L1_xattn_bo"]])[None], (128, 2, D)),
        "w1": i["L0_xattn_W1"], "b1": i["L0_xattn_b1"].reshape(2, 128).T,
        "w2": i["L0_xattn_W2"].reshape(2, 128, D).transpose(1, 0, 2),
        "wo": i["L1_xattn_Wo"],
        "f_int": _np.stack([i["L0_ffn_w_gate"].T, i["L0_ffn_w_up"].T,
                            i["L0_ffn_w_down"].T.reshape(3, 128, D).transpose(1, 0, 2).reshape(128, FH)], 1),
        "ws": i["L1_ffn_Ws"], "bs": row(i["L1_ffn_bs"]),
        "eg": i["L1_ffn_Wg"], "eu": i["L1_ffn_Wu"],
        "ed01": down[:, 0:256].reshape(E, 2, 128, D).transpose(2, 0, 1, 3).reshape(128, E, 2 * D),
        "ed2": down[:, 256:EF].transpose(1, 0, 2),
    }
    arrays = {k: _np.ascontiguousarray(v) for k, v in arrays.items()}
    nc = _bacc.Bacc("TRN2", target_bir_lowering=False, num_devices=1)
    aps = {k: nc.dram_tensor(f"in_{k}", v.shape, _mybir.dt.from_np(v.dtype), kind="ExternalInput").ap()
           for k, v in arrays.items()}
    out = nc.dram_tensor("out", (B, 128, QT, D), _mybir.dt.float32, kind="ExternalOutput").ap()
    flamingo(nc, aps, out)
    got = _run(nc, [{f"in_{k}": v for k, v in arrays.items()}], core_ids=[0]).results[0]["out"]
    return _np.asarray(got).reshape(B, 128, QT, D).transpose(0, 2, 1, 3).reshape(B, T, D)
```

```python
import concourse.bass as bass
from concourse import mybir
from contextlib import ExitStack
import numpy as np

F32 = mybir.dt.float32
F32R = mybir.dt.float32r
I32 = mybir.dt.int32
U32 = mybir.dt.uint32
ALU = mybir.AluOpType
ACT = mybir.ActivationFunctionType
AX = mybir.AxisListType

B, T, D = 2, 512, 128
QT = T // 128
S, C = 154, 96
H, DH = 16, 8
G, J = 4, 4
SM = 128
SR = S - SM
KB = 160
HID = 2 * D
FH = 384
E, EF = 8, 344
FT = [128, 128, EF - 256]
SCALE = DH ** -0.5
CLAMP = 10000.0
FLOOR = 80.0
DEQ = 1.0 / 127.0
EPS = 1e-5

A_BANK, E_BANK, PV_BANK, TR_BANK, G_BANK = (0, 1), (2, 3), 4, 5, (6, 7)


def units():
    return [(l, b, j) for l in range(2) for b in range(B) for j in range(J)]


SKEW = {
    "tensor": {},
    "vector": {"shift": -1.6, "share": 1.0, "values": -3.0},
    "scalar": {"shift": 0.5, "values": 1.2},
    "gpsimd": {},
}
CHAIN = 2.2


def schedule():
    first = {(0, 0): 0, (0, 1): 4, (1, 0): 12, (1, 1): 16}
    out = []

    def put(at, *steps, every=CHAIN):
        for n, step in enumerate(steps):
            out.append((at + n * every, step))

    put(-30, ("norm", 0, 0), ("normed", 0, 0), ("turn", 0, 0), ("query", 0, 0))
    put(2.5, ("norm", 0, 1), ("normed", 0, 1), ("turn", 0, 1), ("query", 0, 1))
    for u, (l, b, j) in enumerate(units()):
        slot = 8 * (first[l, b] + j)
        put(slot, *[("scan", u, k) for k in range(2 * QT)], every=1)
        put(slot + 8 + 1.5, ("shift", u))
        put(slot + 16 + 0.1, *[("exps", u, t) for t in range(5)], every=1)
        put(slot + 24 + 2.1, ("values", u))
        put(slot + 32 + 5.1, ("share", u))
    for b in range(B):
        put(8 * (first[0, b] + 8) - 1.7, ("join", 0, b), ("mlp_up", b, 0), ("mlp_up", b, 1), ("mlp_down", b),
            ("norm", 1, b), ("normed", 1, b), ("turn", 1, b), ("ffn_up", b, 0), ("ffn_up", b, 1),
            ("ffn_up", b, 2), ("ffn_down", b), ("norm", 2, b), ("normed", 2, b), ("turn", 2, b), ("query", 1, b))
        put(8 * (first[1, b] + 8) - 1.7, ("join", 1, b), ("out_proj", b), ("norm", 3, b), ("normed", 3, b),
            ("turn", 3, b), ("route", b))
    for b in range(B):
        put(1000 * (b + 1), *[(kind, e, b) for e in range(E) for kind in ("expert_up", "expert_down")])
    return out


def ordered(timed, engine):
    skew = SKEW[engine]
    return [step for _, step in sorted(timed, key=lambda x: x[0] + skew.get(x[1][0], 0))]


def turns(steps, users):
    out, n = {}, 0
    for step in steps:
        if step[0] in users:
            out[step] = n
            n += users[step[0]]
    return out


def flamingo(nc, a, out):
    TIMED = schedule()
    STEPS = ordered(TIMED, "tensor")
    UNITS = units()
    SETUP = [("keys", 0), ("values_in", 0), ("values_in", 1), ("keys", 1)]
    g_turn = turns(SETUP + STEPS, {"keys": 1, "values_in": 1, "query": 1, "mlp_up": 1, "mlp_down": 1,
                                   "ffn_up": 2, "ffn_down": 1, "out_proj": 1, "route": 1})
    tr_turn = turns(STEPS, {"shift": 1, "share": 1, "join": 1, "turn": 1})
    norm_no = turns(STEPS, {"norm": 1})
    join_no = turns(STEPS, {"join": 1})
    g_end = sum(g_turn[s] >= 0 for s in g_turn) + sum(s[0] == "ffn_up" for s in STEPS)

    ctx = ExitStack()
    with ctx:
        def sb(name, shape, dt=F32):
            return ctx.enter_context(nc.sbuf_tensor(name, shape, dt))

        def sem(name):
            return ctx.enter_context(nc.semaphore(name))

        x = sb("x", [128, B * QT, D])
        xn = sb("xn", [128, B, QT, D])
        xt = sb("xt", [128, B, T])
        x_hi = sb("x_hi", [128, B, T], F32R)
        x_lo = sb("x_lo", [128, B, T], F32R)
        qk_hi = sb("qk_hi", [128, B, T])
        qk_lo = sb("qk_lo", [128, B, T])
        q_st = [sb("q_st0", [128, B, J, T], F32R), sb("q_st1", [128, B, J, T], F32R)]
        k_st = [sb("k_st0", [128, J, B, G * KB], F32R), sb("k_st1", [128, J, B, G * KB], F32R)]
        v_main = sb("v_main", [128, 2, B, H, DH + 1])
        v_rest = sb("v_rest", [128, 2, B, J, 128])
        ex = sb("ex", [128, 2, 5, T])
        pv = sb("pv", [128, 2, T])
        o_tok = sb("o_tok", [128, B, QT, D])
        o_t = sb("o_t", [128, T])
        hid = sb("hid", [128, 3, T])
        sg = sb("sg", [128, T])
        ctx_t = sb("ctx_t", [C + 1, B, KB])
        head_mask = sb("head_mask", [128, G])
        ctx_r = sb("ctx_r", [C + 1, B, G, 32])
        wk = sb("wk", [C + 1, 2, D])
        wv = sb("wv", [C + 1, 2, D])
        wq = sb("wq", [128, 2, D])
        bq = sb("bq", [128, 2])
        w1 = sb("w1", [128, HID])
        b1 = sb("b1", [128, 2])
        w2 = sb("w2", [128, 2, D])
        wo = sb("wo", [128, D])
        bias_out = sb("bias_out", [128, 2, D])
        f_w = sb("f_w", [128, 3, FH])
        ident = sb("ident", [128, 128])
        iota = sb("iota", [128, E])
        bs = sb("bs", [128, E])
        ws = sb("ws", [128, E])
        raw = sb("raw", [128, 4, EF])
        f_int = raw[:].rearrange("p n f -> p (n f)")[:, 0:3 * FH].bitcast(I32).rearrange("p (n f) -> p n f", n=3)
        eg_hi = sb("eg_hi", [128, E, EF], F32R)
        eu_hi = sb("eu_hi", [128, E, EF], F32R)
        eg_lo = k_st[0][:].rearrange("p j b c -> p (j b c)")[:, 0:E * EF].rearrange("p (e f) -> p e f", e=E)
        eu_lo = q_st[0][:].rearrange("p b j t -> p (b j t)")[:, 0:E * EF].rearrange("p (e f) -> p e f", e=E)
        ed = sb("ed", [128, E, 3, D])
        gate_in = sb("gate_in", [128, 4])
        gate = sb("gate", [128, 4])
        stats = sb("stats", [128, B, QT, 6])
        mv = sb("mv", [128, B, QT, 2])
        rstd = sb("rstd", [128, B, QT])
        mhalf = sb("mhalf", [128, QT])
        mx = sb("mx", [128, 2, QT, G])
        mx_parts = sb("mx_parts", [128, 2, QT, 2, G])
        rden = sb("rden", [128, QT, G])
        logit = sb("logit", [128, QT, E])
        top = sb("top", [128, QT, 8])
        top_i = sb("top_i", [128, QT, 8], U32)
        top_f = sb("top_f", [128, QT, 2])
        dl = sb("dl", [128, 3, QT])
        tw = sb("tw", [128, 2, QT])
        pick = sb("pick", [128, 2, QT, E])
        comb = sb("comb", [128, B, QT, E])
        ps = ctx.enter_context(nc.psum_tensor("ps", [128, 8, 512], F32))

        KW = B * KB
        set_up = [ex[:, l, :, :].rearrange("p t c -> p (t c)") for l in range(2)]
        k_hi = [set_up[l][:, 0:KW] for l in range(2)]
        k_lo = [set_up[l][:, KW:2 * KW] for l in range(2)]
        k_rows = [set_up[l][:, 2 * KW:2 * KW + J * KW].rearrange("p (j c) -> p j c", j=J) for l in range(2)]

        ld_ctx, ld_x, ld_q, ld_const, ld_vr = (sem(n) for n in ("ld_ctx", "ld_x", "ld_q", "ld_const", "ld_vr"))
        ld_mlp, ld_ffn, ld_moe, ld_gate = (sem(n) for n in ("ld_mlp", "ld_ffn", "ld_moe", "ld_gate"))
        ld_raw = [sem(f"ld_raw{n}") for n in range(4)]
        zeroed = sem("zeroed")
        zeroed_rest = sem("zeroed_rest")
        ctx_ready = sem("ctx_ready")
        rows_one = sem("rows_one")
        k_hi_done = sem("k_hi_done")
        k_in = [sem(f"k_in{l}") for l in range(2)]
        k_ready = [sem(f"k_ready{l}") for l in range(2)]
        w_ready = sem("w_ready")
        tanh_done = sem("tanh_done")
        a_full, a_read = sem("a_full"), sem("a_read")
        e_full, e_read = sem("e_full"), sem("e_read")
        pv_full, pv_read = sem("pv_full"), sem("pv_read")
        tr_full, tr_read = sem("tr_full"), sem("tr_read")
        g_full = [sem("g_full0"), sem("g_full1")]
        g_read = [sem("g_read0"), sem("g_read1")]
        q_hi_done = sem("q_hi_done")
        q_in = [sem(f"q_in{n}") for n in range(2 * B)]
        max_split = sem("max_split")
        clamped = sem("clamped")
        join_read = sem("join_read")
        var_done, rstd_done, xn_done = sem("var_done"), sem("rstd_done"), sem("xn_done")
        halves_hi, halves_done = sem("halves_hi"), sem("halves_done")
        biased = sem("biased")
        silu_done = sem("silu_done")
        gap_done, e_gap = sem("gap_done"), sem("e_gap")
        routed = sem("routed")
        chain = sem("chain")
        pool_chain = sem("pool_chain")
        split_done = sem("split_done")
        eg_full, eu_full, ed_full = sem("eg_full"), sem("eu_full"), sem("ed_full")
        e_silu, e_hid, e_added = sem("e_silu"), sem("e_hid"), sem("e_added")
        stored = sem("stored")

        def g_bank(turn):
            return ps[:, G_BANK[turn % 2], :]

        def wait_g_free(eng, turn):
            if turn >= 2:
                eng.wait_ge(g_read[turn % 2], turn // 2)

        def wait_g_full(eng, turn):
            eng.wait_ge(g_full[turn % 2], turn // 2 + 1)

        def wait_g_read(eng, turn):
            eng.wait_ge(g_read[turn % 2], turn // 2 + 1)

        tr = ps[:, TR_BANK, :]

        def stack_keys(engine, l, j):
            for first, to, width in ((0, 0, SM), (SM, G * SM, 32)):
                keys = k_rows[l][:, j, :].rearrange("p (b c) -> p b c", b=B)[:, :, first:first + width]
                last = engine.tensor_tensor(
                    k_st[l][:, j, :, to:to + G * width].rearrange("p b (g c) -> p b g c", g=G),
                    keys.unsqueeze(2).broadcast_to([128, B, G, width]),
                    head_mask[:].unsqueeze(1).unsqueeze(3).broadcast_to([128, B, G, width]), ALU.mult)
            return last

        LAST = len(UNITS)

        block = ctx.enter_context(nc.Block())

        @block.sync
        def _(sp):
            sp.dma_start(ctx_t[0:C, :, 0:S], a["ctx_t"]).then_inc(ld_ctx, 16)
            sp.dma_start(wk[:, :, :], a["wk"]).then_inc(ld_ctx, 16)
            sp.dma_start(wv[:, :, :], a["wv"]).then_inc(ld_ctx, 16)
            for b in range(B):
                sp.dma_start(x[:, b * QT:(b + 1) * QT, :], a["x"][b]).then_inc(ld_x, 16)
            sp.dma_start(v_rest[:].rearrange("p l b j c -> p (l b j) c"), a["v_rest0"]).then_inc(ld_vr, 16)
            def load_keys(l):
                wait_g_read(sp, g_turn[("keys", l)])
                for r, src in enumerate((k_hi[l], k_hi[l], k_lo[l])):
                    sp.dma_start(k_rows[l][32 * r:32 * r + 32, :, :], src).then_inc(k_in[l], 16)

            load_keys(0)
            for step in STEPS:
                if step[0] == "query":
                    _, l, b = step
                    wait_g_read(sp, g_turn[step])
                    for r, src in enumerate((qk_hi, qk_lo, qk_hi)):
                        sp.dma_start(q_st[l][32 * r:32 * r + 32, b, :, :].bitcast(F32), src[:, b, :])\
                            .then_inc(q_in[l * B + b], 16)
                    if (l, b) == (0, 0):
                        load_keys(1)
            for b in range(B):
                sp.wait_ge(e_added, E * (b + 1))
                sp.dma_start(out[b], x[:, b * QT:(b + 1) * QT, :]).then_inc(stored, 16)
            sp.wait_ge(stored, 16 * B)

        @block.gpsimd
        def _(pool):
            nc.gpsimd.memset(q_st[0][96:128, 1, :, :].bitcast(U32), 0).then_inc(zeroed_rest, 1)
            pool.wait_ge(zeroed_rest, 1)
            nc.gpsimd.memset(q_st[1][96:128, :, :, :].bitcast(U32), 0).then_inc(zeroed_rest, 1)
            links = [0]

            def link(ins):
                links[0] += 1
                ins.then_inc(pool_chain, 1)
                pool.wait_ge(pool_chain, links[0])

            weights = [(w, e) for w in range(2) for e in range(E)]

            def load_raw(n):
                w, e = weights[n]
                nc.gpsimd.dma_start(raw[:, n % 4, :], a[("eg", "eu")[w]][e]).then_inc(ld_raw[n % 4], 16)

            def split(n):
                w, e = weights[n]
                hi, lo = (eg_hi, eu_hi)[w], (eg_lo, eu_lo)[w]
                pool.wait_ge(ld_raw[n % 4], 16 * (n // 4 + 1))
                link(nc.gpsimd.tensor_copy(hi[:, e, :], raw[:, n % 4, :]))
                nc.gpsimd.tensor_tensor(lo[:, e, :], raw[:, n % 4, :], hi[:, e, :].bitcast(F32),
                                        ALU.subtract).then_inc(split_done, 1)

            pool.wait_ge(ld_const, 32)
            pool.wait_ge(rows_one, 1)
            pool.wait_ge(zeroed_rest, 2)
            splits = 0
            for step in ordered(TIMED, "gpsimd"):
                if step[0] == "norm":
                    _, i, b = step
                    pool.wait_ge(var_done, norm_no[step] + 1)
                    link(nc.gpsimd.tensor_scalar(rstd[:, b, :], mv[:, b, :, 1], EPS, None, ALU.add))
                    nc.gpsimd.tensor_tensor(rstd[:, b, :], rstd[:, b, :], mhalf[:], ALU.pow).then_inc(rstd_done, 1)
                if step[0] == "normed":
                    _, i, b = step
                    if i in (0, 2):
                        pool.wait_ge(xn_done, norm_no[("norm", i, b)] + 1)
                        pool.wait_ge(w_ready, 1)
                        xb = x[:, b * QT:(b + 1) * QT, :]
                        nc.gpsimd.tensor_tensor(xb, xb, bias_out[:, i // 2:i // 2 + 1, :].broadcast_to([128, QT, D]),
                                                ALU.add).then_inc(biased, 1)
                    if (i, b) == (0, 1):
                        pool.wait_ge(k_in[1], 16 * 3)
                        pool.wait_ge(rows_one, 1)
                        for j in range(J):
                            stack_keys(nc.gpsimd, 1, j).then_inc(k_ready[1], 1)
                if step[0] == "exps" and step[2] == 4 and step[1] >= B * J - 1 and splits < len(weights):
                    if splits == 0:
                        pool.wait_ge(e_full, 5 * B * J)
                        pool.wait_ge(w_ready, 2)
                        for n in range(4):
                            load_raw(n)
                    for n in range(splits, splits + 2):
                        split(n)
                    for n in range(splits + 4, min(splits + 6, len(weights))):
                        pool.wait_ge(split_done, n - 3)
                        load_raw(n)
                    splits += 2

        @block.scalar
        def _(act):
            act.dma_start(ident[:], a["ident"]).then_inc(ld_const, 16)
            act.dma_start(head_mask[:], a["head_mask"]).then_inc(ld_const, 16)
            act.dma_start(wq[:], a["wq"]).then_inc(ld_q, 16)
            act.dma_start(bq[:], a["bq"]).then_inc(ld_q, 16)
            act.dma_start(gate_in[:], a["gates"]).then_inc(ld_gate, 16)
            act.dma_start(bias_out[:], a["bias_out"]).then_inc(ld_gate, 16)
            act.dma_start(w1[:], a["w1"]).then_inc(ld_mlp, 16)
            act.dma_start(b1[:], a["b1"]).then_inc(ld_mlp, 16)
            act.dma_start(w2[:], a["w2"]).then_inc(ld_mlp, 16)
            act.dma_start(f_int, a["f_int"]).then_inc(ld_ffn, 16)
            act.dma_start(wo[:], a["wo"]).then_inc(ld_moe, 16)
            act.dma_start(iota[:], a["iota"]).then_inc(ld_moe, 16)
            act.dma_start(bs[:], a["bs"]).then_inc(ld_moe, 16)
            act.dma_start(ws[:], a["ws"]).then_inc(ld_moe, 16)
            act.dma_start(ed[:, :, 0:2, :].rearrange("p e t d -> p e (t d)"), a["ed01"]).then_inc(ld_moe, 16)
            act.dma_start(ed[0:FT[2], :, 2, :], a["ed2"]).then_inc(ld_moe, 16)
            act.wait_ge(ld_gate, 32)
            nc.scalar.activation(gate[:], gate_in[:], ACT.Tanh).then_inc(tanh_done, 1)
            for step in SETUP:
                if step[0] == "keys":
                    l = step[1]
                    turn = g_turn[step]
                    wait_g_full(act, turn)
                    nc.scalar.activation(k_hi[l].bitcast(F32R), g_bank(turn)[:, 0:KW], ACT.Copy)\
                        .then_inc(k_hi_done, 1)
            ups = 0
            for step in ordered(TIMED, "scalar"):
                kind = step[0]
                if kind == "query":
                    _, l, b = step
                    turn = g_turn[step]
                    wait_g_full(act, turn)
                    if l:
                        act.wait_ge(q_in[b], 16 * 3)
                    act.wait_ge(w_ready, 1)
                    nc.scalar.activation(qk_hi[:, b, :].bitcast(F32R), g_bank(turn), ACT.Identity,
                                         bias=bq[:, l:l + 1]).then_inc(q_hi_done, 1)
                elif kind == "shift":
                    u = step[1]
                    act.wait_ge(tr_full, tr_turn[step] + 1)
                    l, b, j = UNITS[u]
                    nc.scalar.copy(q_st[l][96:96 + 2 * G, b, j, :], tr[0:2 * G, :]).then_inc(tr_read, 1)
                elif kind == "exps":
                    _, u, t = step
                    n = 5 * u + t
                    if t == 0 and u < 2:
                        act.wait_ge(k_ready[u], J)
                    if t == 0 and u >= 2:
                        act.wait_ge(pv_full, u - 1)
                    act.wait_ge(e_full, n + 1)
                    nc.scalar.activation(ex[:, u % 2, t, :], ps[:, E_BANK[n % 2], :], ACT.Exp).then_inc(e_read, 1)
                elif kind == "values":
                    u = step[1]
                    act.wait_ge(pv_full, u + 1)
                    if u >= 2:
                        act.wait_ge(tr_full, tr_turn[("share", u - 2)] + 1)
                    nc.scalar.copy(pv[:, u % 2, :], ps[:, PV_BANK, :]).then_inc(pv_read, 1)
                elif kind == "join":
                    n = join_no[step]
                    act.wait_ge(tr_full, tr_turn[step] + 1)
                    if n >= 1:
                        before = [s for s in STEPS if s[0] == "join"][n - 1]
                        if before[1] == 0:
                            wait_g_full(act, g_turn[("mlp_up", before[2], 1)])
                        else:
                            wait_g_full(act, g_turn[("out_proj", before[2])])
                    nc.scalar.copy(o_t[:], tr).then_inc(tr_read, 1)
                elif kind == "turn":
                    _, i, b = step
                    act.wait_ge(tr_full, tr_turn[step] + 1)
                    nc.scalar.copy(xt[:, b, :], tr).then_inc(tr_read, 1)
                    if i == 3:
                        act.wait_ge(tr_read, tr_turn[step] + 1)
                        nc.scalar.copy(x_hi[:, b, :], xt[:, b, :]).then_inc(halves_hi, 1)
                elif kind == "mlp_up":
                    _, b, f = step
                    turn = g_turn[step]
                    wait_g_full(act, turn)
                    if b:
                        wait_g_full(act, g_turn[("ffn_down", b - 1)])
                    nc.scalar.activation(hid[:, f, :], g_bank(turn), ACT.Relu, bias=b1[:, f:f + 1])\
                        .then_inc(g_read[turn % 2], 1)
                elif kind == "ffn_up":
                    _, b, f = step
                    turn = g_turn[step]
                    wait_g_full(act, turn)
                    if ups:
                        wait_g_read(act, last_up + 1)
                    nc.scalar.activation(sg[:], g_bank(turn), ACT.Silu).then_inc(g_read[turn % 2], 1)
                    last_up = turn
                    ups += 1
                elif kind == "route":
                    b = step[1]
                    act.wait_ge(gap_done, b + 1)
                    nc.scalar.activation(dl[:, 1, :], dl[:, 0, :], ACT.Exp).then_inc(e_gap, 1)
                elif kind == "expert_up":
                    _, e, b = step
                    for f, rows in enumerate(FT):
                        n = (b * E + e) * 3 + f
                        act.wait_ge(eg_full, n + 1)
                        if n >= 2:
                            act.wait_ge(e_hid, n - 1)
                        else:
                            act.wait_ge(pv_full, LAST)
                        nc.scalar.activation(ex[0:rows, n % 2, 3, :], ps[0:rows, (0, 1)[n % 2], :], ACT.Silu)\
                            .then_inc(e_silu, 1)

        @block.vector
        def _(dve):
            links = [0]

            def link(ins):
                links[0] += 1
                ins.then_inc(chain, 1)
                dve.wait_ge(chain, links[0])

            nc.vector.memset(mhalf[:], -0.5)
            link(nc.vector.memset(ctx_t[:, :, S:KB], 0.0))
            link(nc.vector.memset(ctx_t[C:C + 1, :, 0:S], 1.0))
            dve.wait_ge(ld_ctx, 48)
            for b in range(B):
                last = nc.vector.tensor_copy(ctx_r[:, b, :, :],
                                             ctx_t[:, b, SM:KB].unsqueeze(1).broadcast_to([C + 1, G, 32]))
            last.then_inc(ctx_ready, 1)
            for l in range(2):
                last = nc.vector.memset(k_rows[l][96:128, :, :], 1.0)
            last.then_inc(rows_one, 1)
            nc.vector.memset(q_st[0][96:128, 0, :, :].bitcast(U32), 0)
            nc.vector.memset(v_main[:], 1.0).then_inc(zeroed, 1)
            dve.wait_ge(ld_q, 32)
            nc.vector.tensor_scalar(wq[:], wq[:], SCALE, None, ALU.mult)
            nc.vector.tensor_scalar(bq[:], bq[:], SCALE, None, ALU.mult)
            dve.wait_ge(tanh_done, 1)
            for l in range(2):
                last = nc.vector.tensor_scalar(bias_out[:, l, :], bias_out[:, l, :], gate[:, l:l + 1], None, ALU.mult)
            last.then_inc(w_ready, 1)
            for step in SETUP:
                turn = g_turn[step]
                wait_g_full(dve, turn)
                if step[0] == "keys":
                    l = step[1]
                    dve.wait_ge(k_hi_done, l + 1)
                    nc.vector.tensor_tensor(k_lo[l].bitcast(F32R), g_bank(turn)[:, 0:KW], k_hi[l],
                                            ALU.subtract).then_inc(g_read[turn % 2], 1)
                else:
                    b = step[1]
                    if b == 0:
                        dve.wait_ge(ld_vr, 16)
                        dve.wait_ge(zeroed, 1)
                    bank = g_bank(turn)
                    nc.vector.tensor_copy(v_main[:, :, b, :, 0:DH],
                                          bank[:, 0:2 * D].rearrange("p (l h d) -> p l h d", l=2, h=H))
                    for g in range(G):
                        for l in range(2):
                            rows = slice(32 * g, 32 * g + 32)
                            first = 2 * D + l * D + 32 * g
                            last = nc.vector.tensor_copy(
                                v_rest[rows, l, b, :, 32 * g:32 * g + DH],
                                bank[rows, first:first + 32].rearrange("p (j d) -> p j d", j=J))
                    last.then_inc(g_read[turn % 2], 1)

            def stack_layer_0():
                dve.wait_ge(ld_const, 32)
                dve.wait_ge(k_in[0], 16 * 3)
                dve.wait_ge(rows_one, 1)
                for j in range(J):
                    stack_keys(nc.vector, 0, j).then_inc(k_ready[0], 1)
                dve.wait_ge(ld_ffn, 16)
                nc.vector.tensor_scalar(f_w[:], f_int, DEQ, None, ALU.mult).then_inc(w_ready, 1)

            for step in ordered(TIMED, "vector"):
                kind = step[0]
                if kind == "norm":
                    _, i, b = step
                    if i == 0:
                        dve.wait_ge(ld_x, 16 * B)
                    elif i in (1, 3):
                        wait_g_read(dve, g_turn[("mlp_down", b) if i == 1 else ("out_proj", b)])
                    else:
                        wait_g_read(dve, g_turn[("ffn_down", b)])
                    for q in range(QT):
                        last = nc.vector.bn_stats(stats[:, b, q, :], x[:, b * QT + q, :])
                    link(last)
                    for q in range(QT):
                        last = nc.vector.bn_aggr(mv[:, b, q, :], stats[:, b, q, :])
                    last.then_inc(var_done, 1)
                elif kind == "normed":
                    _, i, b = step
                    dve.wait_ge(rstd_done, norm_no[("norm", i, b)] + 1)
                    dve.wait_ge(var_done, norm_no[("norm", i, b)] + 1)
                    if i:
                        dve.wait_ge(tr_full, tr_turn[("turn", i - 1, b)] + 1)
                    for q in range(QT):
                        last = nc.vector.tensor_scalar(xn[:, b, q, :], x[:, b * QT + q, :], mv[:, b, q, 0:1],
                                                       rstd[:, b, q:q + 1], ALU.subtract, ALU.mult)
                    last.then_inc(xn_done, 1)
                elif kind == "turn":
                    _, i, b = step
                    if i == 3:
                        dve.wait_ge(halves_hi, b + 1)
                        nc.vector.tensor_tensor(x_lo[:, b, :], xt[:, b, :], x_hi[:, b, :].bitcast(F32),
                                                ALU.subtract).then_inc(halves_done, 1)
                elif kind == "query":
                    _, l, b = step
                    turn = g_turn[step]
                    dve.wait_ge(q_hi_done, l * B + b + 1)
                    nc.vector.scalar_tensor_tensor(qk_lo[:, b, :].bitcast(F32R), g_bank(turn), bq[:, l:l + 1],
                                                   qk_hi[:, b, :], ALU.add, ALU.subtract)\
                        .then_inc(g_read[turn % 2], 1)
                    if (l, b) == (0, 0):
                        stack_layer_0()
                elif kind == "scan":
                    _, u, k = step
                    n = 2 * QT * u + k
                    dve.wait_ge(a_full, n + 1)
                    nc.vector.tensor_reduce(mx[:, u % 2, k // 2, 2 * (k % 2):2 * (k % 2) + 2],
                                            ps[:, A_BANK[n % 2], 0:2 * S].rearrange("p (h s) -> p h s", h=2),
                                            AX.X, ALU.max).then_inc(a_read, 1)
                elif kind == "shift":
                    u = step[1]
                    dve.wait_ge(a_read, 2 * QT * (u + 1))
                    m = mx[:, u % 2, :, :]
                    if UNITS[u][0] == 1:
                        link(nc.vector.tensor_scalar(m, m, FLOOR - CLAMP, CLAMP, ALU.max, ALU.min))
                    if u >= 2:
                        dve.wait_ge(tr_full, tr_turn[("shift", u - 2)] + 1)
                    link(nc.vector.tensor_copy(mx_parts[:, u % 2, :, 0, :].bitcast(F32R), m))
                    nc.vector.tensor_tensor(mx_parts[:, u % 2, :, 1, :].bitcast(F32R), m,
                                            mx_parts[:, u % 2, :, 0, :], ALU.subtract).then_inc(max_split, 1)
                elif kind == "values":
                    u = step[1]
                    if UNITS[u][0] == 1:
                        dve.wait_ge(e_read, 5 * (u + 1))
                        w = ex[:, u % 2, :, :]
                        nc.vector.tensor_scalar(w, w, float(np.exp(-FLOOR)), 1.0, ALU.max, ALU.min)\
                            .then_inc(clamped, 1)
                elif kind == "share":
                    u = step[1]
                    l, b, j = UNITS[u]
                    dve.wait_ge(tr_full, tr_turn[step] + 1)
                    t4 = tr.rearrange("p (q g c) -> p q g c", q=QT, g=G)
                    link(nc.vector.reciprocal(rden[:], t4[:, :, :, DH]))
                    if l and j == 0:
                        dve.wait_ge(tr_full, tr_turn[("join", 0, b)] + 1)
                    nc.vector.tensor_tensor(
                        o_tok[:, b, :, :].rearrange("p q (g j d) -> p q g j d", g=G, j=J)[:, :, :, j, :],
                        t4[:, :, :, 0:DH], rden[:].unsqueeze(3).broadcast_to([128, QT, G, DH]),
                        ALU.mult).then_inc(tr_read, 1)
                elif kind in ("mlp_down", "out_proj", "ffn_down"):
                    b = step[1]
                    turn = g_turn[step]
                    wait_g_full(dve, turn)
                    col = {"mlp_down": 0, "out_proj": 1, "ffn_down": 2}[kind]
                    if kind != "ffn_down":
                        norm_before = [s for s in STEPS if s[0] == "norm" and s[1] in (0, 2)]
                        dve.wait_ge(biased, norm_before.index(("norm", 2 * col, b)) + 1)
                    xb = x[:, b * QT:(b + 1) * QT, :].rearrange("p q d -> p (q d)")
                    nc.vector.scalar_tensor_tensor(xb, g_bank(turn), gate[:, col:col + 1], xb, ALU.mult, ALU.add)\
                        .then_inc(g_read[turn % 2], 1)
                elif kind == "ffn_up":
                    _, b, f = step
                    turn = g_turn[step]
                    wait_g_read(dve, turn)
                    wait_g_full(dve, turn + 1)
                    nc.vector.tensor_tensor(hid[:, f, :], sg[:], g_bank(turn + 1), ALU.mult)\
                        .then_inc(g_read[(turn + 1) % 2], 1)
                elif kind == "route":
                    b = step[1]
                    turn = g_turn[step]
                    if b == 0:
                        dve.wait_ge(ld_moe, 16 * 6)
                    wait_g_full(dve, turn)
                    bank = g_bank(turn)[:, 0:QT * E].rearrange("p (q e) -> p q e", q=QT)
                    nc.vector.tensor_tensor(logit[:], bank, bs[:].unsqueeze(1).broadcast_to([128, QT, E]),
                                            ALU.add).then_inc(g_read[turn % 2], 1)
                    wait_g_read(dve, turn)
                    for q in range(QT):
                        last = nc.vector.max(top[:, q, :], logit[:, q, :])
                    link(last)
                    for q in range(QT):
                        last = nc.vector.max_index(top_i[:, q, :], top[:, q, :], logit[:, q, :])
                    link(last)
                    nc.vector.tensor_tensor(dl[:, 0, :], top[:, :, 1], top[:, :, 0], ALU.subtract)\
                        .then_inc(gap_done, 1)
                    link(nc.vector.tensor_copy(top_f[:], top_i[:, :, 0:2]))
                    dve.wait_ge(e_gap, b + 1)
                    link(nc.vector.tensor_scalar(dl[:, 2, :], dl[:, 1, :], 1.0, None, ALU.add))
                    link(nc.vector.reciprocal(tw[:, 0, :], dl[:, 2, :]))
                    link(nc.vector.tensor_scalar(tw[:, 0, :], tw[:, 0, :], gate[:, 3:4], None, ALU.mult))
                    link(nc.vector.tensor_tensor(tw[:, 1, :], tw[:, 0, :], dl[:, 1, :], ALU.mult))
                    for n in range(2):
                        link(nc.vector.tensor_tensor(pick[:, n, :, :], iota[:].unsqueeze(1).broadcast_to([128, QT, E]),
                                                     top_f[:, :, n:n + 1].broadcast_to([128, QT, E]), ALU.is_equal))
                        link(nc.vector.tensor_tensor(pick[:, n, :, :], pick[:, n, :, :],
                                                     tw[:, n, :].unsqueeze(2).broadcast_to([128, QT, E]), ALU.mult))
                    nc.vector.tensor_tensor(comb[:, b, :, :], pick[:, 0, :, :], pick[:, 1, :, :], ALU.add)\
                        .then_inc(routed, 1)
                elif kind == "expert_up":
                    _, e, b = step
                    for f, rows in enumerate(FT):
                        n = (b * E + e) * 3 + f
                        dve.wait_ge(e_silu, n + 1)
                        dve.wait_ge(eu_full, n + 1)
                        if f == 0 and n >= 6:
                            dve.wait_ge(ed_full, b * E + e - 1)
                        nc.vector.tensor_tensor(ex[0:rows, (b * E + e) % 2, f, :], ex[0:rows, n % 2, 3, :],
                                                ps[0:rows, (2, 3)[n % 2], :], ALU.mult).then_inc(e_hid, 1)
                elif kind == "expert_down":
                    _, e, b = step
                    n = b * E + e
                    dve.wait_ge(ed_full, n + 1)
                    dve.wait_ge(routed, b + 1)
                    if e:
                        dve.wait_ge(e_added, n)
                    for q in range(QT):
                        xb = x[:, b * QT + q, :]
                        last = nc.vector.scalar_tensor_tensor(xb, ps[:, (4, 5)[n % 2], q * D:(q + 1) * D],
                                                              comb[:, b, q, e:e + 1], xb, ALU.mult, ALU.add)
                    last.then_inc(e_added, 1)

        @block.tensor
        def _(pe):
            def mm(o, lhsT, rhs, start=True, stop=True):
                return nc.tensor.matmul(o, lhsT, rhs, start=start, stop=stop, skip_group_check=True)

            pe.wait_ge(ctx_ready, 1)
            for step in SETUP:
                turn = g_turn[step]
                wait_g_free(pe, turn)
                bank = g_bank(turn)
                if step[0] == "keys":
                    last = mm(bank[:, 0:KW], wk[:, step[1], :], ctx_t[:].rearrange("c b s -> c (b s)"))
                else:
                    b = step[1]
                    mm(bank[:, 0:2 * D], ctx_t[:, b, 0:SM], wv[:].rearrange("c l d -> c (l d)"))
                    last = mm(bank[:, 2 * D:4 * D], ctx_r[:, b, :, :].rearrange("c g k -> c (g k)"),
                              wv[:].rearrange("c l d -> c (l d)"))
                last.then_inc(g_full[turn % 2], 1)
            pe.wait_ge(ld_const, 32)
            for step in ordered(TIMED, "tensor"):
                kind = step[0]
                if kind == "turn":
                    _, i, b = step
                    turn = tr_turn[step]
                    pe.wait_ge(xn_done, norm_no[("norm", i, b)] + 1)
                    if turn:
                        pe.wait_ge(tr_read, turn)
                    for q in range(QT):
                        last = nc.tensor.transpose(tr[:, q * 128:(q + 1) * 128], xn[:, b, q, :], ident[:])
                    last.then_inc(tr_full, 1)
                elif kind == "query":
                    _, l, b = step
                    turn = g_turn[step]
                    wait_g_free(pe, turn)
                    pe.wait_ge(w_ready, 1)
                    pe.wait_ge(tr_read, tr_turn[("turn", 2 * l, b)] + 1)
                    mm(g_bank(turn), wq[:, l, :], xt[:, b, :]).then_inc(g_full[turn % 2], 1)
                elif kind == "scan":
                    _, u, k = step
                    l, b, j = UNITS[u]
                    n = 2 * QT * u + k
                    if k == 0 and j == 0:
                        pe.wait_ge(q_in[l * B + b], 16 * 3)
                        if (l, b) == (0, 0):
                            pe.wait_ge(zeroed, 1)
                        else:
                            pe.wait_ge(zeroed_rest, 1 + l)
                    if k == 0 and b == 0:
                        pe.wait_ge(k_ready[l], j + 1)
                    if n >= 2:
                        pe.wait_ge(a_read, n - 1)
                    half = k % 2
                    queries = q_st[l][:, b, j, (k // 2) * 128:(k // 2 + 1) * 128]
                    o = ps[:, A_BANK[n % 2], 0:2 * S].rearrange("p (h s) -> p h s", h=2)
                    rest = k_st[l][:, j, b, SM * G + 64 * half:SM * G + 64 * (half + 1)]
                    mm(o[:, :, 0:SM], queries, k_st[l][:, j, b, 2 * SM * half:2 * SM * (half + 1)])
                    mm(o[:, :, SM:S], queries, rest.rearrange("p (h s) -> p h s", h=2)[:, :, 0:SR])\
                        .then_inc(a_full, 1)
                elif kind == "shift":
                    u = step[1]
                    turn = tr_turn[step]
                    pe.wait_ge(max_split, u + 1)
                    if turn:
                        pe.wait_ge(tr_read, turn)
                    for q in range(QT):
                        last = nc.tensor.transpose(tr[0:2 * G, q * 128:(q + 1) * 128],
                                                   mx_parts[:, u % 2, q, :, :].rearrange("p a g -> p (a g)"), ident[:])
                    last.then_inc(tr_full, 1)
                elif kind == "exps":
                    _, u, t = step
                    l, b, j = UNITS[u]
                    n = 5 * u + t
                    if t == 0:
                        pe.wait_ge(tr_read, tr_turn[("shift", u)] + 1)
                    if n >= 2:
                        pe.wait_ge(e_read, n - 1)
                    first = SM * G if t == 0 else SM * (t - 1)
                    keys = k_st[l][:, j, b, first:first + SM]
                    mm(ps[:, E_BANK[n % 2], :], keys, q_st[l][:, b, j, :]).then_inc(e_full, 1)
                elif kind == "values":
                    u = step[1]
                    l, b, j = UNITS[u]
                    if l:
                        pe.wait_ge(clamped, u - B * J + 1)
                    else:
                        pe.wait_ge(e_read, 5 * (u + 1))
                    if u:
                        pe.wait_ge(pv_read, u)
                    mm(ps[:, PV_BANK, :], v_rest[:, l, b, j, :], ex[:, u % 2, 0, :], stop=False)
                    for g in range(G):
                        last = mm(ps[32 * g:32 * g + DH + 1, PV_BANK, :], v_main[:, l, b, J * g + j, :],
                                  ex[:, u % 2, 1 + g, :], start=False)
                    last.then_inc(pv_full, 1)
                elif kind == "share":
                    u = step[1]
                    turn = tr_turn[step]
                    pe.wait_ge(pv_read, u + 1)
                    pe.wait_ge(tr_read, turn)
                    for q in range(QT):
                        last = nc.tensor.transpose(tr[:, q * 128:(q + 1) * 128], pv[:, u % 2, q * 128:(q + 1) * 128],
                                                   ident[:])
                    last.then_inc(tr_full, 1)
                elif kind == "join":
                    _, l, b = step
                    turn = tr_turn[step]
                    pe.wait_ge(tr_read, turn)
                    for q in range(QT):
                        last = nc.tensor.transpose(tr[:, q * 128:(q + 1) * 128], o_tok[:, b, q, :], ident[:])
                    last.then_inc(tr_full, 1)
                elif kind == "mlp_up":
                    _, b, f = step
                    turn = g_turn[step]
                    if f == 0:
                        pe.wait_ge(ld_mlp, 48)
                        pe.wait_ge(tr_read, tr_turn[("join", 0, b)] + 1)
                    wait_g_free(pe, turn)
                    mm(g_bank(turn), w1[:, f * 128:(f + 1) * 128], o_t[:]).then_inc(g_full[turn % 2], 1)
                elif kind == "mlp_down":
                    b = step[1]
                    turn = g_turn[step]
                    for f in range(2):
                        wait_g_read(pe, g_turn[("mlp_up", b, f)])
                    wait_g_free(pe, turn)
                    for q in range(QT):
                        for f in range(2):
                            last = mm(g_bank(turn)[:, q * D:(q + 1) * D], hid[:, f, q * 128:(q + 1) * 128],
                                      w2[:, f, :], start=(f == 0), stop=(f == 1))
                    last.then_inc(g_full[turn % 2], 1)
                elif kind == "out_proj":
                    b = step[1]
                    turn = g_turn[step]
                    pe.wait_ge(ld_moe, 16 * 6)
                    pe.wait_ge(tr_read, tr_turn[("join", 1, b)] + 1)
                    wait_g_free(pe, turn)
                    for q in range(QT):
                        last = mm(g_bank(turn)[:, q * D:(q + 1) * D], o_t[:, q * 128:(q + 1) * 128], wo[:])
                    last.then_inc(g_full[turn % 2], 1)
                elif kind == "ffn_up":
                    _, b, f = step
                    turn = g_turn[step]
                    if f == 0:
                        pe.wait_ge(w_ready, 2)
                        pe.wait_ge(tr_read, tr_turn[("turn", 1, b)] + 1)
                    for n in range(2):
                        wait_g_free(pe, turn + n)
                        mm(g_bank(turn + n), f_w[:, n, f * 128:(f + 1) * 128], xt[:, b, :])\
                            .then_inc(g_full[(turn + n) % 2], 1)
                elif kind == "ffn_down":
                    b = step[1]
                    turn = g_turn[step]
                    for f in range(3):
                        wait_g_read(pe, g_turn[("ffn_up", b, f)] + 1)
                    wait_g_free(pe, turn)
                    for q in range(QT):
                        for f in range(3):
                            last = mm(g_bank(turn)[:, q * D:(q + 1) * D], hid[:, f, q * 128:(q + 1) * 128],
                                      f_w[:, 2, f * 128:(f + 1) * 128], start=(f == 0), stop=(f == 2))
                    last.then_inc(g_full[turn % 2], 1)
                elif kind == "route":
                    b = step[1]
                    turn = g_turn[step]
                    pe.wait_ge(tr_read, tr_turn[("turn", 3, b)] + 1)
                    wait_g_free(pe, turn)
                    for q in range(QT):
                        last = mm(g_bank(turn)[:, q * E:(q + 1) * E], xt[:, b, q * 128:(q + 1) * 128], ws[:])
                    last.then_inc(g_full[turn % 2], 1)
                elif kind == "expert_up":
                    _, e, b = step
                    if e == 0:
                        pe.wait_ge(halves_done, b + 1)
                        pe.wait_ge(split_done, 2 * E)
                        if b == 0:
                            pe.wait_ge(a_read, 2 * QT * LAST)
                            pe.wait_ge(e_read, 5 * LAST)
                            pe.wait_ge(pv_read, LAST)
                            pe.wait_ge(tr_read, len(tr_turn))
                    for f, rows in enumerate(FT):
                        n = (b * E + e) * 3 + f
                        cols = slice(f * 128, f * 128 + rows)
                        for hi, lo, bank, full, used in ((eg_hi, eg_lo, (0, 1), eg_full, e_silu),
                                                         (eu_hi, eu_lo, (2, 3), eu_full, e_hid)):
                            if n >= 2:
                                pe.wait_ge(used, n - 1)
                            o = ps[0:rows, bank[n % 2], :]
                            mm(o, hi[:, e, cols], x_hi[:, b, :], stop=False)
                            mm(o, hi[:, e, cols], x_lo[:, b, :], start=False, stop=False)
                            mm(o, lo[:, e, cols], x_hi[:, b, :], start=False).then_inc(full, 1)
                elif kind == "expert_down":
                    _, e, b = step
                    n = b * E + e
                    pe.wait_ge(e_hid, 3 * (n + 1))
                    if n >= 2:
                        pe.wait_ge(e_added, n - 1)
                    for q in range(QT):
                        for f, rows in enumerate(FT):
                            last = mm(ps[:, (4, 5)[n % 2], q * D:(q + 1) * D],
                                      ex[0:rows, n % 2, f, q * 128:(q + 1) * 128], ed[0:rows, e, f, :],
                                      start=(f == 0), stop=(f == 2))
                    last.then_inc(ed_full, 1)


def kernel(**inputs):
    import numpy as _np
    import concourse.bacc as _bacc
    from concourse import mybir as _mybir
    from concourse.bass_utils import run_bass_kernel_spmd as _run

    i = {k: _np.asarray(v) for k, v in inputs.items()}
    tok = lambda v: v.reshape(B, QT, 128, D).transpose(0, 2, 1, 3)
    heads = lambda v: v.reshape(-1, G, J, DH).transpose(0, 1, 3, 2).reshape(-1, D)
    row = lambda v, n=128: _np.broadcast_to(v.reshape(1, -1), (n, v.size))
    ctx_rows = lambda w, b: _np.concatenate([w, b.reshape(1, -1)], 0)
    head_mask = _np.zeros((128, G), _np.float32)
    for g in range(G):
        for r in range(3):
            head_mask[32 * r + DH * g:32 * r + DH * (g + 1), g] = 1.0
        head_mask[[96 + g, 96 + G + g], g] = -1.0
    v_rest0 = _np.zeros((128, 128), _np.float32)
    for g in range(G):
        v_rest0[32 * g:32 * g + SR, 32 * g + DH] = 1.0
    down = i["L1_ffn_Wd"]
    arrays = {
        "x": tok(i["x"]),
        "ctx_t": i["ctx_768"].transpose(2, 0, 1),
        "wk": _np.stack([ctx_rows(heads(i[f"L{l}_xattn_Wk"]), heads(i[f"L{l}_xattn_bk"])) for l in range(2)], 1),
        "wv": _np.stack([ctx_rows(i[f"L{l}_xattn_Wv"], i[f"L{l}_xattn_bv"]) for l in range(2)], 1),
        "wq": _np.stack([heads(i[f"L{l}_xattn_Wq"]) for l in range(2)], 1),
        "bq": _np.stack([heads(i[f"L{l}_xattn_bq"])[0] for l in range(2)], 1),
        "v_rest0": _np.broadcast_to(v_rest0[:, None, :], (128, 2 * B * J, 128)),
        "head_mask": head_mask,
        "ident": _np.eye(128, dtype=_np.float32),
        "iota": row(_np.arange(E, dtype=_np.float32)),
        "gates": row(_np.concatenate([i["g_xattn"], i["g_ffn"]])),
        "bias_out": _np.broadcast_to(_np.stack([i["L0_xattn_b2"], i["L1_xattn_bo"]])[None], (128, 2, D)),
        "w1": i["L0_xattn_W1"], "b1": i["L0_xattn_b1"].reshape(2, 128).T,
        "w2": i["L0_xattn_W2"].reshape(2, 128, D).transpose(1, 0, 2),
        "wo": i["L1_xattn_Wo"],
        "f_int": _np.stack([i["L0_ffn_w_gate"].T, i["L0_ffn_w_up"].T,
                            i["L0_ffn_w_down"].T.reshape(3, 128, D).transpose(1, 0, 2).reshape(128, FH)], 1),
        "ws": i["L1_ffn_Ws"], "bs": row(i["L1_ffn_bs"]),
        "eg": i["L1_ffn_Wg"], "eu": i["L1_ffn_Wu"],
        "ed01": down[:, 0:256].reshape(E, 2, 128, D).transpose(2, 0, 1, 3).reshape(128, E, 2 * D),
        "ed2": down[:, 256:EF].transpose(1, 0, 2),
    }
    arrays = {k: _np.ascontiguousarray(v) for k, v in arrays.items()}
    nc = _bacc.Bacc("TRN2", target_bir_lowering=False, num_devices=1)
    aps = {k: nc.dram_tensor(f"in_{k}", v.shape, _mybir.dt.from_np(v.dtype), kind="ExternalInput").ap()
           for k, v in arrays.items()}
    out = nc.dram_tensor("out", (B, 128, QT, D), _mybir.dt.float32, kind="ExternalOutput").ap()
    flamingo(nc, aps, out)
    got = _run(nc, [{f"in_{k}": v for k, v in arrays.items()}], core_ids=[0]).results[0]["out"]
    return _np.asarray(got).reshape(B, 128, QT, D).transpose(0, 2, 1, 3).reshape(B, T, D)
```

```python
import concourse.bass as bass
from concourse import mybir
from contextlib import ExitStack
import numpy as np

F32 = mybir.dt.float32
F32R = mybir.dt.float32r
I32 = mybir.dt.int32
U32 = mybir.dt.uint32
ALU = mybir.AluOpType
ACT = mybir.ActivationFunctionType
AX = mybir.AxisListType

B, T, D = 2, 512, 128
QT = T // 128
S, C = 154, 96
H, DH = 16, 8
G, J = 4, 4
SM = 128
SR = S - SM
KB = 160
HID = 2 * D
FH = 384
E, EF = 8, 344
FP = 352
ET = E * FP // 128
CHUNK = 384
CHUNKS = -(-ET * 128 // CHUNK)
RING = 4
SCALE = DH ** -0.5
CLAMP = 10000.0
FLOOR = 80.0
DEQ = 1.0 / 127.0
EPS = 1e-5

A_BANK, E_BANK, PV_BANK, TR_BANK, G_BANK = (0, 1), (2, 3), 4, 5, (6, 7)


def units():
    return [(l, b, j) for l in range(2) for b in range(B) for j in range(J)]


UNIT_LAYER = [l for l, _, _ in units()]

SKEW = {
    "tensor": {},
    "vector": {
        "ffn_down": 1.72, "norm": -0.19, "shift0": -1.63, "shift1": -1.57, "share0": 1.0, "share1": 1.0,
        "clamp1": 0.48, "turn": 0.73, "scan0": -0.9, "scan1": -0.23, "query": 1.65, "ffn_up": -0.27,
        "mlp_down": -1.35,
    },
    "scalar": {},
    "gpsimd": {},
}
FIRST = {(0, 0): 0, (0, 1): 4, (1, 0): 11.25, (1, 1): 15.75}
AFTER = [
    {
        "scan": [-0.04, 1.01, 1.34, 2.85, 3.5, 4.5, 5.84, 7.79], "shift": 9.35,
        "exps": [11.4, 11.52, 13.84, 14.18, 14.7], "rests": 16.12, "values": 17.97, "share": 20.9,
    },
    {
        "scan": [0.2, 1.4, 2.4, 3.19, 3.63, 5.39, 6.31, 7.53], "shift": 9.41,
        "exps": [11.16, 12.92, 13.77, 14.6, 15.8], "clamp": [13.41, 15, 16.04], "rests": 16.84,
        "values": 19.01, "share": 24.15,
    },
]
CHAINS = {
    (0, 0): [
        17.13, 2.16, 2.16, 2.1, 2.16, 3.0, 2.32, 2.16, 1.7, 2.16, 2.03, 6.4, 1.97, 3.46, 1.87, 4.7,
    ],
    (0, 1): [
        17.3, 2.3, 2.16, 2.16, 2.16, 2.16, 2.16, 2.16, 2.39, 2.16, 2.37, 2.51, 1.33, 2.16, 4.87, 1.05,
    ],
    (1, 0): [
        25.37, 2.4, 2.4, 2.24, 2.4, 2.4, 2.4,
    ],
    (1, 1): [
        20.02, 2.15, 2.15, 1.99, 2.15, 2.15, 2.15,
    ],
}
EXPERTS = 21.55
SPLIT_SLOT = 11.65
SET_UP = {
    "scale_q": -49, "norm1": -38.8, "stack0": -26.5, "ctx_r": -22.09, "normed1": -24.2, "turn1": -14.14,
    "query1": 3.7, "keys1": 8.75, "v_ones": -23.04, "values0": 13.54, "values1": 27.31, "gates": 19.0,
    "ffn_w": 44.4, "stack": -8.2, "stack1": 26.31,
}
WEIGH, DOWN = 1.73, 2.5
SPLITS = 2.42
TILE = 2.59


def schedule():
    out = []

    def put(at, *steps, every=2.2):
        for n, step in enumerate(steps):
            out.append((at + n * every, step))

    put(-50, ("norm", 0, 0), ("keys", 0), ("normed", 0, 0), ("turn", 0, 0), ("query", 0, 0))
    for name, *steps in (("scale_q", ("scale_q",)), ("norm1", ("norm", 0, 1)), ("stack0", ("stack", 0, 0)),
                         ("ctx_r", ("ctx_r",)), ("normed1", ("normed", 0, 1)), ("turn1", ("turn", 0, 1)),
                         ("query1", ("query", 0, 1)),
                         ("keys1", ("keys", 1)), ("v_ones", ("v_ones",)), ("values0", ("values_in", 0)),
                         ("values1", ("values_in", 1)), ("gates", ("gates",), ("bias", 0, 0), ("bias", 0, 1)),
                         ("ffn_w", ("ffn_w",))):
        put(SET_UP[name], *steps)
    for j in range(1, J):
        put(8 * j + SET_UP["stack"], ("stack", 0, j))
    put(SET_UP["stack1"], *[("stack", 1, j) for j in range(J)], every=5)
    for u, (l, b, j) in enumerate(units()):
        slot = 8 * (FIRST[l, b] + j)
        for name, after in AFTER[l].items():
            if type(after) is list:
                for n, at in enumerate(after):
                    put(slot + at, (name, u, n))
            else:
                put(slot + after, (name, u))
    for b in range(B):
        steps = (
            (("join", 0, b), ("mlp_up", b, 0), ("mlp_up", b, 1), ("mlp_down", b), ("norm", 1, b), ("normed", 1, b),
             ("turn", 1, b), ("ffn_up", b, 0), ("ffn_up", b, 1), ("ffn_up", b, 2), ("ffn_down", b), ("norm", 2, b),
             ("normed", 2, b), ("turn", 2, b), ("query", 1, b), ("bias", 2, b)),
            (("join", 1, b), ("out_proj", b), ("norm", 3, b), ("normed", 3, b), ("turn", 3, b), ("route", b),
             ("comb", b)))
        for l in range(2):
            at = 8 * (FIRST[l, b] + J)
            for step, gap in zip(steps[l], CHAINS[l, b]):
                at += gap
                put(at, step)
    put(8 * SPLIT_SLOT, *[("split", n) for n in range(3 * CHUNKS)], every=SPLITS)
    for n in range(B * ET):
        at = 8 * EXPERTS + n * TILE
        put(at, ("up", n))
        put(at + TILE * WEIGH, ("weigh", n))
        put(at + TILE * DOWN, ("down", n))
    for b in range(B):
        put(8 * EXPERTS + ((b + 1) * ET + 3.2) * TILE, ("finish", b))
    return out


def experts_of(t):
    parts = []
    for row in range(4):
        e = hidden_block(t, row)[0]
        if parts and parts[-1][0] == e:
            parts[-1] = (e, parts[-1][1], 32 * row + 32)
        else:
            parts.append((e, 32 * row, 32 * row + 32))
    return parts


def hidden_block(t, row):
    turned = (row + 1) % 4 if t % 11 == 8 else row
    return divmod(4 * t + turned, FP // 32)


def ordered(timed, engine):
    skew = SKEW[engine]
    by_layer = ("scan", "shift", "exps", "clamp", "rests", "values", "share")

    def time(x):
        at, step = x
        return at + skew.get(step[0] + (str(UNIT_LAYER[step[1]]) if step[0] in by_layer else ""), 0)

    return [step for _, step in sorted(timed, key=time)]


def turns(steps, users):
    out, n = {}, 0
    for step in steps:
        if step[0] in users:
            out[step] = n
            n += users[step[0]]
    return out


def flamingo(nc, a, comb_rows, out):
    TIMED = schedule()
    STEPS = ordered(TIMED, "tensor")
    UNITS = units()
    g_turn = turns(STEPS, {"keys": 1, "values_in": 1, "query": 1, "mlp_up": 1, "mlp_down": 1,
                                   "ffn_up": 2, "ffn_down": 1, "out_proj": 1, "route": 1})
    tr_turn = turns(STEPS, {"shift": 1, "share": 1, "join": 1, "turn": 1, "comb": 1, "finish": 1})
    norm_no = turns(STEPS, {"norm": 1})
    normed_no = turns(STEPS, {"normed": 1})
    bias_no = turns(STEPS, {"bias": 1})
    join_no = turns(STEPS, {"join": 1})

    ctx = ExitStack()
    with ctx:
        def sb(name, shape, dt=F32):
            return ctx.enter_context(nc.sbuf_tensor(name, shape, dt))

        def sem(name):
            return ctx.enter_context(nc.semaphore(name))

        x = sb("x", [128, B * QT, D])
        xn = sb("xn", [128, B, QT, D])
        xt = sb("xt", [128, B, T])
        x_hi = sb("x_hi", [128, B, T], F32R)
        x_lo = sb("x_lo", [128, B, T], F32R)
        qk_hi = sb("qk_hi", [128, B, T])
        qk_lo = sb("qk_lo", [128, B, T])
        q_st = [sb("q_st0", [128, B, J, T], F32R), sb("q_st1", [128, B, J, T], F32R)]
        k_st = [sb("k_st0", [128, J, B, G * KB], F32R), sb("k_st1", [128, J, B, G * KB], F32R)]
        v_main = sb("v_main", [128, 2, B, H, DH + 1])
        is_rest = sb("is_rest", [128, 1])
        v_rest = sb("v_rest", [128, 2, B, J, 128])
        ex = sb("ex", [128, 2, 5, T])
        pv = sb("pv", [128, 2, T])
        o_tok = sb("o_tok", [128, B, QT, D])
        o_t = sb("o_t", [128, T])
        hid = sb("hid", [128, 3, T])
        sg = sb("sg", [128, T])
        ctx_t = sb("ctx_t", [C + 1, B, KB])
        head_mask = sb("head_mask", [128, G])
        ctx_r = sb("ctx_r", [C + 1, B, G, 32])
        wk = sb("wk", [C + 1, 2, D])
        wv = sb("wv", [C + 1, 2, D])
        wq = sb("wq", [128, 2, D])
        bq = sb("bq", [128, 2])
        w1 = sb("w1", [128, HID])
        b1 = sb("b1", [128, 2])
        w2 = sb("w2", [128, 2, D])
        wo = sb("wo", [128, D])
        bias_out = sb("bias_out", [128, 2, D])
        f_w = sb("f_w", [128, 3, FH])
        ident = sb("ident", [128, 128])
        iota = sb("iota", [128, E])
        bs = sb("bs", [128, E])
        ws = sb("ws", [128, E])
        raw = sb("raw", [128, 4, CHUNK])
        f_int = raw[:].rearrange("p n f -> p (n f)")[:, 0:3 * FH].bitcast(I32).rearrange("p (n f) -> p n f", n=3)
        w_hi = [sb(name, [128, ET * 128], F32R) for name in ("eg_hi", "eu_hi", "ed_hi")]
        room = [st[:].rearrange("p a b c -> p (a b c)") for st in (k_st[0], q_st[0])]
        comb_t = sb("comb_t", [E, B, T])
        comb_row = q_st[1][:, 0, :, :].bitcast(F32)
        h_silu = [t[:, 0, :, :].rearrange("p q d -> p (q d)") for t in (xn, o_tok)]
        h_all = [hid[:, n, :] for n in range(3)] + [sg[:]]
        h_hi = [half[:, n, :].bitcast(F32R) for half in (qk_lo, qk_hi) for n in range(2)]
        h_lo = [q_st[1][:, 1, n, :] for n in range(RING)]
        gate_in = sb("gate_in", [128, 4])
        gate = sb("gate", [128, 4])
        stats = sb("stats", [128, B, QT, 6])
        mv = sb("mv", [128, B, QT, 2])
        rstd = sb("rstd", [128, B, QT])
        mhalf = sb("mhalf", [128, QT])
        mx = sb("mx", [128, 2, QT, G])
        mx_parts = sb("mx_parts", [128, 2, QT, 2, G])
        rden = sb("rden", [128, QT, G])
        logit = sb("logit", [128, QT, E])
        top = sb("top", [128, QT, 8])
        top_i = sb("top_i", [128, QT, 8], U32)
        top_f = sb("top_f", [128, QT, 2])
        dl = sb("dl", [128, 3, QT])
        tw = sb("tw", [128, 2, QT])
        pick = sb("pick", [128, 2, QT, E])
        comb = sb("comb", [128, B, QT, E])
        ps = ctx.enter_context(nc.psum_tensor("ps", [128, 8, 512], F32))

        KW = B * KB
        set_up = [q_st[1][:, l, :, :].rearrange("p j t -> p (j t)").bitcast(F32) for l in range(2)]
        k_hi = [set_up[l][:, 0:KW] for l in range(2)]
        k_lo = [set_up[l][:, KW:2 * KW] for l in range(2)]
        k_rows = [set_up[l][:, 2 * KW:2 * KW + J * KW].rearrange("p (j c) -> p j c", j=J) for l in range(2)]

        ld_ctx, ld_v, ld_q, ld_ident, ld_mask = (sem(f"ld_{n}") for n in ("ctx", "v", "q", "ident", "mask"))
        ld_rest = sem("ld_rest")
        ld_x = [sem(f"ld_x{b}") for b in range(B)]
        ld_mlp, ld_ffn, ld_moe, ld_gate = (sem(n) for n in ("ld_mlp", "ld_ffn", "ld_moe", "ld_gate"))
        ld_raw = [sem(f"ld_raw{n}") for n in range(4)]
        half_there = sem("half_there")
        ctx_padded = sem("ctx_padded")
        ctx_ready = sem("ctx_ready")
        zeroed = sem("zeroed")
        rows_one = [sem(f"rows_one{l}") for l in range(2)]
        k_hi_done = sem("k_hi_done")
        k_in = [sem(f"k_in{l}") for l in range(2)]
        k_ready = [sem(f"k_ready{l}") for l in range(2)]
        q_scaled, bias_scaled, f_ready = sem("q_scaled"), sem("bias_scaled"), sem("f_ready")
        tanh_done, ffn_tanh = sem("tanh_done"), sem("ffn_tanh")
        a_full, a_read = sem("a_full"), sem("a_read")
        e_full, e_read = sem("e_full"), sem("e_read")
        pv_full, pv_read = sem("pv_full"), sem("pv_read")
        tr_full, tr_read = sem("tr_full"), sem("tr_read")
        g_full = [sem("g_full0"), sem("g_full1")]
        g_read = [sem("g_read0"), sem("g_read1")]
        q_hi_done = sem("q_hi_done")
        q_in = [sem(f"q_in{n}") for n in range(2 * B)]
        max_split = sem("max_split")
        clamped = sem("clamped")
        var_done, rstd_done, xn_done = sem("var_done"), sem("rstd_done"), sem("xn_done")
        halves_hi, halves_done = sem("halves_hi"), sem("halves_done")
        biased = sem("biased")
        gap_done, e_gap = sem("gap_done"), sem("e_gap")
        routed = sem("routed")
        chain = sem("chain")
        pool_chain = sem("pool_chain")
        split_hi, split_lo = sem("split_hi"), sem("split_lo")
        eg_full, eu_full = sem("eg_full"), sem("eu_full")
        e_silu, e_hid = sem("e_silu"), sem("e_hid")
        weighed, last_weighed = sem("weighed"), sem("last_weighed")
        h_hi_done, h_lo_done = sem("h_hi_done"), sem("h_lo_done")
        y_added = sem("y_added")
        y_read = sem("y_read")
        comb_out = sem("comb_out")
        comb_in = [sem(f"comb_in{n}") for n in range(RING)]
        stored = sem("stored")

        def g_bank(turn):
            return ps[:, G_BANK[turn % 2], :]

        def wait_g_free(eng, turn):
            if turn >= 2:
                eng.wait_ge(g_read[turn % 2], turn // 2)

        def wait_g_full(eng, turn):
            eng.wait_ge(g_full[turn % 2], turn // 2 + 1)

        def wait_g_read(eng, turn):
            eng.wait_ge(g_read[turn % 2], turn // 2 + 1)

        tr = ps[:, TR_BANK, :]

        def w_lo(w, first, last):
            base = (0, 0, ET * 128)[w]
            if w == 1 or w == 2 and first >= 6 * CHUNK:
                return room[1][:, base - 6 * CHUNK * (w == 2) + first:base - 6 * CHUNK * (w == 2) + last]
            return room[0][:, base + first:base + last]

        def halves(n):
            w, c = n // CHUNKS, n % CHUNKS
            first, last = c * CHUNK, min((c + 1) * CHUNK, ET * 128)
            return w_hi[w][:, first:last], w_lo(w, first, last)

        Y_BANK = (PV_BANK, G_BANK[0])
        G_TURNS = 1 + max(g_turn.values())

        def last_tile_of(e):
            return max(t for t in range(ET) if e in [part[0] for part in experts_of(t)])

        def stack_keys(engine, l, j):
            for first, to, width in ((0, 0, SM), (SM, G * SM, 32)):
                keys = k_rows[l][:, j, :].rearrange("p (b c) -> p b c", b=B)[:, :, first:first + width]
                last = engine.tensor_tensor(
                    k_st[l][:, j, :, to:to + G * width].rearrange("p b (g c) -> p b g c", g=G),
                    keys.unsqueeze(2).broadcast_to([128, B, G, width]),
                    head_mask[:].unsqueeze(1).unsqueeze(3).broadcast_to([128, B, G, width]), ALU.mult)
            return last

        LAST = len(UNITS)

        block = ctx.enter_context(nc.Block())

        @block.sync
        def _(sp):
            sp.dma_start(x[:, 0:QT, :], a["x"][0]).then_inc(ld_x[0], 16)
            sp.dma_start(ctx_t[0:C, :, 0:S], a["ctx_t"]).then_inc(ld_ctx, 16)
            sp.dma_start(wk[:, :, :], a["wk"]).then_inc(ld_ctx, 16)
            sp.dma_start(x[:, QT:2 * QT, :], a["x"][1]).then_inc(ld_x[1], 16)

            def load_raw(n):
                w, c = n // CHUNKS, n % CHUNKS
                last = min((c + 1) * CHUNK, ET * 128)
                sp.dma_start(raw[:, n % 4, 0:last - c * CHUNK], a["experts"][:, w, c * CHUNK:last])\
                    .then_inc(ld_raw[n % 4], 16)

            for step in STEPS:
                if step[0] == "split":
                    n = step[1]
                    if n == 0:
                        sp.wait_ge(f_ready, 1)
                        for m in range(3):
                            load_raw(m)
                    if n + 3 < 3 * CHUNKS:
                        if n >= 1:
                            sp.wait_ge(split_lo, n)
                        load_raw(n + 3)
                if step[0] == "keys":
                    l = step[1]
                    wait_g_read(sp, g_turn[step])
                    for r, src in enumerate((k_hi[l], k_hi[l], k_lo[l])):
                        sp.dma_start(k_rows[l][32 * r:32 * r + 32, :, :], src).then_inc(k_in[l], 16)
                if step[0] == "query":
                    _, l, b = step
                    wait_g_read(sp, g_turn[step])
                    for r, src in enumerate((qk_hi, qk_lo, qk_hi)):
                        sp.dma_start(q_st[l][32 * r:32 * r + 32, b, :, :].bitcast(F32), src[:, b, :])\
                            .then_inc(q_in[l * B + b], 16)
                    if (l, b) == (0, 1):
                        sp.dma_start(gate_in[:], a["gates"]).then_inc(ld_gate, 16)
                        sp.dma_start(bias_out[:], a["bias_out"]).then_inc(ld_gate, 16)
                        sp.dma_start(f_int, a["f_int"]).then_inc(ld_ffn, 16)
                        sp.dma_start(w1[:], a["w1"]).then_inc(ld_mlp, 16)
                        sp.dma_start(b1[:], a["b1"]).then_inc(ld_mlp, 16)
                        sp.dma_start(w2[:], a["w2"]).then_inc(ld_mlp, 16)
                        sp.dma_start(wo[:], a["wo"]).then_inc(ld_moe, 16)
                        sp.dma_start(iota[:], a["iota"]).then_inc(ld_moe, 16)
                        sp.dma_start(bs[:], a["bs"]).then_inc(ld_moe, 16)
                        sp.dma_start(ws[:], a["ws"]).then_inc(ld_moe, 16)
            sp.wait_ge(e_full, 5 * (LAST - J))
            for n in range(B * E):
                b, e = n // E, n % E
                if e == 0:
                    sp.wait_ge(tr_read, tr_turn[("comb", b)] + 1)
                    sp.dma_start(comb_rows[b], comb_t[:, b, :]).then_inc(comb_out, 16)
                    sp.wait_ge(comb_out, 16 * (b + 1))
                if n >= RING:
                    before = n - RING
                    sp.wait_ge(weighed, before // E * ET + last_tile_of(before % E) + 1)
                sp.dma_start(comb_row[:, n % RING, :], comb_rows[b, e:e + 1, :].broadcast_to([128, T]))\
                    .then_inc(comb_in[n % RING], 16)
            for b in range(B):
                sp.wait_ge(tr_read, tr_turn[("finish", b)] + 1)
                sp.dma_start(out[b], x[:, b * QT:(b + 1) * QT, :]).then_inc(stored, 16)
            sp.wait_ge(stored, 16 * B)

        @block.gpsimd
        def _(pool):
            nc.gpsimd.memset(q_st[0][96:128, :, :, :].bitcast(U32), 0).then_inc(zeroed, 1)
            pool.wait_ge(zeroed, 1)
            nc.gpsimd.memset(k_rows[1][96:128, :, :].bitcast(U32), 0x3F800000).then_inc(rows_one[1], 1)
            links = [0]

            def link(ins):
                links[0] += 1
                ins.then_inc(pool_chain, 1)
                pool.wait_ge(pool_chain, links[0])

            pool.wait_ge(half_there, 1)
            pool.wait_ge(rows_one[1], 1)
            for step in ordered(TIMED, "gpsimd"):
                if step[0] == "norm":
                    _, i, b = step
                    pool.wait_ge(var_done, norm_no[step] + 1)
                    link(nc.gpsimd.tensor_scalar(rstd[:, b, :], mv[:, b, :, 1], EPS, None, ALU.add))
                    nc.gpsimd.tensor_tensor(rstd[:, b, :], rstd[:, b, :], mhalf[:], ALU.pow).then_inc(rstd_done, 1)
                    if (i, b) == (0, 0):
                        nc.gpsimd.memset(v_rest[:], 0.0).then_inc(zeroed, 1)
                if step[0] == "bias":
                    _, i, b = step
                    pool.wait_ge(xn_done, QT * (normed_no[("normed", i, b)] + 1))
                    pool.wait_ge(bias_scaled, 1)
                    xb = x[:, b * QT:(b + 1) * QT, :]
                    nc.gpsimd.tensor_tensor(xb, xb, bias_out[:, i // 2:i // 2 + 1, :].broadcast_to([128, QT, D]),
                                            ALU.add).then_inc(biased, 1)
                if step[0] == "stack" and step[1] == 1:
                    j = step[2]
                    if j == 0:
                        pool.wait_ge(k_in[1], 16 * 3)
                        pool.wait_ge(ld_mask, 16)
                    stack_keys(nc.gpsimd, 1, j).then_inc(k_ready[1], 1)
                    if j == J - 1:
                        for l in range(2):
                            pool.wait_ge(k_ready[l], J)
                        nc.gpsimd.memset(q_st[1][96:128, :, :, :].bitcast(U32), 0).then_inc(zeroed, 1)
                        pool.wait_ge(zeroed, 3)
                if step[0] == "split":
                    n = step[1]
                    pool.wait_ge(split_hi, n + 1)
                    if n == 0:
                        pool.wait_ge(e_full, 5 * B * J)
                    hi, lo = halves(n)
                    nc.gpsimd.tensor_tensor(lo, raw[:, n % 4, 0:lo.shape[1]], hi.bitcast(F32), ALU.subtract)\
                        .then_inc(split_lo, 1)
                if step[0] == "weigh" and step[1] < B * ET - 1:
                    n = step[1]
                    b, t = n // ET, n % ET
                    pool.wait_ge(e_hid, n + 1)
                    if n:
                        pool.wait_ge(weighed, n)
                    for e, first, last in experts_of(t):
                        if first:
                            link(ins)
                        m = b * E + e
                        pool.wait_ge(comb_in[m % RING], 16 * (m // RING + 1))
                        h = h_all[n % RING][first:last, :]
                        ins = nc.gpsimd.tensor_tensor(h, h, comb_row[first:last, m % RING, :], ALU.mult)
                    ins.then_inc(weighed, 1)

        @block.scalar
        def _(act):
            act.dma_start(ident[:], a["ident"]).then_inc(ld_ident, 16)
            act.dma_start(wq[:], a["wq"]).then_inc(ld_q, 16)
            act.dma_start(bq[:], a["bq"]).then_inc(ld_q, 16)
            act.dma_start(head_mask[:], a["head_mask"]).then_inc(ld_mask, 16)
            act.dma_start(is_rest[:], a["is_rest"]).then_inc(ld_rest, 16)
            act.dma_start(wv[:], a["wv"]).then_inc(ld_v, 16)
            act.wait_ge(half_there, 1)
            nc.scalar.activation(dl[:, 1, :], mhalf[:], ACT.Exp)
            ups = 0
            for step in ordered(TIMED, "scalar"):
                kind = step[0]
                if kind == "keys":
                    l = step[1]
                    turn = g_turn[step]
                    wait_g_full(act, turn)
                    nc.scalar.copy(k_hi[l].bitcast(F32R), g_bank(turn)[:, 0:KW]).then_inc(k_hi_done, 1)
                elif kind == "gates":
                    act.wait_ge(ld_gate, 32)
                    nc.scalar.activation(gate[:], gate_in[:], ACT.Tanh).then_inc(tanh_done, 1)
                elif kind == "query":
                    _, l, b = step
                    turn = g_turn[step]
                    wait_g_full(act, turn)
                    if l:
                        act.wait_ge(q_in[b], 16 * 3)
                    act.wait_ge(q_scaled, 1)
                    nc.scalar.activation(qk_hi[:, b, :].bitcast(F32R), g_bank(turn), ACT.Identity,
                                         bias=bq[:, l:l + 1]).then_inc(q_hi_done, 1)
                elif kind == "shift":
                    u = step[1]
                    act.wait_ge(tr_full, tr_turn[step] + 1)
                    l, b, j = UNITS[u]
                    nc.scalar.copy(q_st[l][96:96 + 2 * G, b, j, :], tr[0:2 * G, :]).then_inc(tr_read, 1)
                elif kind == "exps":
                    _, u, t = step
                    n = 5 * u + t
                    if t == 0 and u >= 2:
                        act.wait_ge(pv_full, u - 1)
                    act.wait_ge(e_full, n + 1)
                    nc.scalar.activation(ex[:, u % 2, t, :], ps[:, E_BANK[n % 2], :], ACT.Exp).then_inc(e_read, 1)
                elif kind == "values":
                    u = step[1]
                    act.wait_ge(pv_full, u + 1)
                    if u >= 2:
                        act.wait_ge(tr_full, tr_turn[("share", u - 2)] + 1)
                    nc.scalar.copy(pv[:, u % 2, :], ps[:, PV_BANK, :]).then_inc(pv_read, 1)
                elif kind == "join":
                    n = join_no[step]
                    act.wait_ge(tr_full, tr_turn[step] + 1)
                    if n >= 1:
                        before = [s for s in STEPS if s[0] == "join"][n - 1]
                        if before[1] == 0:
                            wait_g_full(act, g_turn[("mlp_up", before[2], 1)])
                        else:
                            wait_g_full(act, g_turn[("out_proj", before[2])])
                    nc.scalar.copy(o_t[:], tr).then_inc(tr_read, 1)
                elif kind == "turn":
                    _, i, b = step
                    act.wait_ge(tr_full, tr_turn[step] + 1)
                    nc.scalar.copy(xt[:, b, :], tr).then_inc(tr_read, 1)
                    if i == 3:
                        act.wait_ge(tr_read, tr_turn[step] + 1)
                        nc.scalar.copy(x_hi[:, b, :], xt[:, b, :]).then_inc(halves_hi, 1)
                elif kind == "mlp_up":
                    _, b, f = step
                    turn = g_turn[step]
                    wait_g_full(act, turn)
                    if b:
                        wait_g_full(act, g_turn[("ffn_down", b - 1)])
                    nc.scalar.activation(hid[:, f, :], g_bank(turn), ACT.Relu, bias=b1[:, f:f + 1])\
                        .then_inc(g_read[turn % 2], 1)
                elif kind == "ffn_up":
                    _, b, f = step
                    turn = g_turn[step]
                    wait_g_full(act, turn)
                    if ups:
                        wait_g_read(act, last_up + 1)
                    nc.scalar.activation(sg[:], g_bank(turn), ACT.Tanh, scale=0.5).then_inc(ffn_tanh, 1)
                    last_up = turn
                    ups += 1
                elif kind == "route":
                    b = step[1]
                    act.wait_ge(gap_done, b + 1)
                    nc.scalar.activation(dl[:, 1, :], dl[:, 0, :], ACT.Exp).then_inc(e_gap, 1)
                elif kind == "split":
                    n = step[1]
                    act.wait_ge(ld_raw[n % 4], 16 * (n // 4 + 1))
                    hi, _ = halves(n)
                    nc.scalar.copy(hi, raw[:, n % 4, 0:hi.shape[1]]).then_inc(split_hi, 1)
                elif kind == "comb":
                    act.wait_ge(tr_full, tr_turn[step] + 1)
                    nc.scalar.copy(comb_t[:, step[1], :], tr[0:E, :]).then_inc(tr_read, 1)
                elif kind == "up":
                    n = step[1]
                    act.wait_ge(eg_full, n + 1)
                    if n >= 2:
                        act.wait_ge(e_hid, n - 1)
                    elif n == 0:
                        act.wait_ge(tr_full, tr_turn[("turn", 3, 0)] + 1)
                        act.wait_ge(tr_full, tr_turn[("join", 1, 0)] + 1)
                    nc.scalar.activation(h_silu[n % 2], ps[:, A_BANK[n % 2], :], ACT.Silu).then_inc(e_silu, 1)
                elif kind == "weigh":
                    n = step[1]
                    if n < B * ET - 1:
                        act.wait_ge(weighed, n + 1)
                    else:
                        act.wait_ge(last_weighed, 1)
                    if n == 0:
                        act.wait_ge(q_in[2 * B - 1], 16 * 3)
                    nc.scalar.copy(h_hi[n % RING], h_all[n % RING]).then_inc(h_hi_done, 1)
                elif kind == "finish":
                    b = step[1]
                    act.wait_ge(y_added, (b + 1) * ET)
                    nc.scalar.copy(pv[:, b, :], ps[:, Y_BANK[b], :]).then_inc(y_read, 1)

        @block.vector
        def _(dve):
            links = [0]

            def link(ins):
                links[0] += 1
                ins.then_inc(chain, 1)
                dve.wait_ge(chain, links[0])

            nc.vector.memset(mhalf[:], -0.5).then_inc(half_there, 1)
            link(nc.vector.memset(ctx_t[:, :, S:KB], 0.0))
            nc.vector.memset(ctx_t[C:C + 1, :, 0:S], 1.0).then_inc(ctx_padded, 1)
            nc.vector.memset(k_rows[0][96:128, :, :].bitcast(U32), 0x3F800000).then_inc(rows_one[0], 1)
            dve_ups = [0]
            for step in ordered(TIMED, "vector"):
                kind = step[0]
                if kind == "keys":
                    l = step[1]
                    turn = g_turn[step]
                    dve.wait_ge(k_hi_done, l + 1)
                    nc.vector.tensor_tensor(k_lo[l].bitcast(F32R), g_bank(turn)[:, 0:KW], k_hi[l],
                                            ALU.subtract).then_inc(g_read[turn % 2], 1)
                elif kind == "stack" and step[1] == 0:
                    j = step[2]
                    if j == 0:
                        dve.wait_ge(ld_mask, 16)
                        dve.wait_ge(k_in[0], 16 * 3)
                        dve.wait_ge(rows_one[0], 1)
                    stack_keys(nc.vector, 0, j).then_inc(k_ready[0], 1)
                elif kind == "scale_q":
                    dve.wait_ge(ld_q, 32)
                    nc.vector.tensor_scalar(wq[:], wq[:], SCALE, None, ALU.mult)
                    nc.vector.tensor_scalar(bq[:], bq[:], SCALE, None, ALU.mult).then_inc(q_scaled, 1)
                elif kind == "ctx_r":
                    dve.wait_ge(ctx_padded, 1)
                    dve.wait_ge(ld_ctx, 32)
                    for b in range(B):
                        last = nc.vector.tensor_copy(ctx_r[:, b, :, :],
                                                     ctx_t[:, b, SM:KB].unsqueeze(1).broadcast_to([C + 1, G, 32]))
                    last.then_inc(ctx_ready, 1)
                elif kind == "v_ones":
                    nc.vector.memset(v_main[:], 1.0)
                    dve.wait_ge(zeroed, 2)
                    dve.wait_ge(ld_rest, 16)
                    for g in range(G):
                        rows = slice(32 * g, 32 * g + 32)
                        ins = nc.vector.tensor_copy(
                            v_rest[rows, :, :, :, 32 * g + DH].rearrange("p l b j -> p (l b j)"),
                            is_rest[rows, :].broadcast_to([32, 2 * B * J]))
                    link(ins)
                elif kind == "values_in":
                    b = step[1]
                    turn = g_turn[step]
                    wait_g_full(dve, turn)
                    bank = g_bank(turn)
                    nc.vector.tensor_copy(v_main[:, :, b, :, 0:DH],
                                          bank[:, 0:2 * D].rearrange("p (l h d) -> p l h d", l=2, h=H))
                    for g in range(G):
                        for l in range(2):
                            rows = slice(32 * g, 32 * g + 32)
                            first = 2 * D + l * D + 32 * g
                            last = nc.vector.tensor_copy(
                                v_rest[rows, l, b, :, 32 * g:32 * g + DH],
                                bank[rows, first:first + 32].rearrange("p (j d) -> p j d", j=J))
                    last.then_inc(g_read[turn % 2], 1)
                elif kind == "gates":
                    dve.wait_ge(tanh_done, 1)
                    for l in range(2):
                        last = nc.vector.tensor_scalar(bias_out[:, l, :], bias_out[:, l, :], gate[:, l:l + 1], None,
                                                       ALU.mult)
                    last.then_inc(bias_scaled, 1)
                elif kind == "ffn_w":
                    dve.wait_ge(ld_ffn, 16)
                    nc.vector.tensor_scalar(f_w[:, 0:2, :], f_int[:, 0:2, :], DEQ, None, ALU.mult)
                    nc.vector.tensor_scalar(f_w[:, 2, :], f_int[:, 2, :], DEQ / 2, None, ALU.mult).then_inc(f_ready, 1)
                elif kind == "norm":
                    _, i, b = step
                    if i == 0:
                        dve.wait_ge(ld_x[b], 16)
                    elif i in (1, 3):
                        wait_g_read(dve, g_turn[("mlp_down", b) if i == 1 else ("out_proj", b)])
                    else:
                        wait_g_read(dve, g_turn[("ffn_down", b)])
                    for q in range(QT):
                        last = nc.vector.bn_stats(stats[:, b, q, :], x[:, b * QT + q, :])
                    link(last)
                    for q in range(QT):
                        last = nc.vector.bn_aggr(mv[:, b, q, :], stats[:, b, q, :])
                    last.then_inc(var_done, 1)
                elif kind == "normed":
                    _, i, b = step
                    dve.wait_ge(rstd_done, norm_no[("norm", i, b)] + 1)
                    dve.wait_ge(var_done, norm_no[("norm", i, b)] + 1)
                    if i:
                        dve.wait_ge(tr_full, tr_turn[("turn", i - 1, b)] + 1)
                    for q in range(QT):
                        nc.vector.tensor_scalar(xn[:, b, q, :], x[:, b * QT + q, :], mv[:, b, q, 0:1],
                                                rstd[:, b, q:q + 1], ALU.subtract, ALU.mult).then_inc(xn_done, 1)
                elif kind == "turn":
                    _, i, b = step
                    if i == 3:
                        dve.wait_ge(halves_hi, b + 1)
                        nc.vector.tensor_tensor(x_lo[:, b, :], xt[:, b, :], x_hi[:, b, :].bitcast(F32),
                                                ALU.subtract).then_inc(halves_done, 1)
                elif kind == "query":
                    _, l, b = step
                    turn = g_turn[step]
                    dve.wait_ge(q_hi_done, l * B + b + 1)
                    nc.vector.scalar_tensor_tensor(qk_lo[:, b, :].bitcast(F32R), g_bank(turn), bq[:, l:l + 1],
                                                   qk_hi[:, b, :], ALU.add, ALU.subtract)\
                        .then_inc(g_read[turn % 2], 1)
                elif kind == "scan":
                    _, u, k = step
                    n = 2 * QT * u + k
                    dve.wait_ge(a_full, n + 1)
                    nc.vector.tensor_reduce(mx[:, u % 2, k // 2, 2 * (k % 2):2 * (k % 2) + 2],
                                            ps[:, A_BANK[n % 2], 0:2 * S].rearrange("p (h s) -> p h s", h=2),
                                            AX.X, ALU.max).then_inc(a_read, 1)
                elif kind == "shift":
                    u = step[1]
                    dve.wait_ge(a_read, 2 * QT * (u + 1))
                    m = mx[:, u % 2, :, :]
                    if UNITS[u][0] == 1:
                        link(nc.vector.tensor_scalar(m, m, FLOOR - CLAMP, CLAMP, ALU.max, ALU.min))
                    if u >= 2:
                        dve.wait_ge(tr_full, tr_turn[("shift", u - 2)] + 1)
                    link(nc.vector.tensor_copy(mx_parts[:, u % 2, :, 0, :].bitcast(F32R), m))
                    nc.vector.tensor_tensor(mx_parts[:, u % 2, :, 1, :].bitcast(F32R), m,
                                            mx_parts[:, u % 2, :, 0, :], ALU.subtract).then_inc(max_split, 1)
                elif kind == "clamp":
                    _, u, n = step
                    dve.wait_ge(e_read, 5 * u + min(2 * n + 2, 5))
                    w = ex[:, u % 2, 2 * n:min(2 * n + 2, 5), :]
                    nc.vector.tensor_scalar(w, w, float(np.exp(-FLOOR)), 1.0, ALU.max, ALU.min).then_inc(clamped, 1)
                elif kind == "share":
                    u = step[1]
                    l, b, j = UNITS[u]
                    dve.wait_ge(tr_full, tr_turn[step] + 1)
                    t4 = tr.rearrange("p (q g c) -> p q g c", q=QT, g=G)
                    link(nc.vector.reciprocal(rden[:], t4[:, :, :, DH]))
                    if l and j == 0:
                        dve.wait_ge(tr_full, tr_turn[("join", 0, b)] + 1)
                    nc.vector.tensor_tensor(
                        o_tok[:, b, :, :].rearrange("p q (g j d) -> p q g j d", g=G, j=J)[:, :, :, j, :],
                        t4[:, :, :, 0:DH], rden[:].unsqueeze(3).broadcast_to([128, QT, G, DH]),
                        ALU.mult).then_inc(tr_read, 1)
                elif kind in ("mlp_down", "out_proj", "ffn_down"):
                    b = step[1]
                    turn = g_turn[step]
                    wait_g_full(dve, turn)
                    col = {"mlp_down": 0, "out_proj": 1, "ffn_down": 2}[kind]
                    if kind != "ffn_down":
                        dve.wait_ge(biased, bias_no[("bias", 2 * col, b)] + 1)
                    xb = x[:, b * QT:(b + 1) * QT, :].rearrange("p q d -> p (q d)")
                    nc.vector.scalar_tensor_tensor(xb, g_bank(turn), gate[:, col:col + 1], xb, ALU.mult, ALU.add)\
                        .then_inc(g_read[turn % 2], 1)
                elif kind == "ffn_up":
                    _, b, f = step
                    turn = g_turn[step]
                    dve_ups[0] += 1
                    dve.wait_ge(ffn_tanh, dve_ups[0])
                    ins = nc.vector.scalar_tensor_tensor(sg[:], sg[:], 1.0, g_bank(turn), ALU.add, ALU.mult)
                    ins.then_inc(g_read[turn % 2], 1)
                    wait_g_read(dve, turn)
                    wait_g_full(dve, turn + 1)
                    nc.vector.tensor_tensor(hid[:, f, :], sg[:], g_bank(turn + 1), ALU.mult)\
                        .then_inc(g_read[(turn + 1) % 2], 1)
                elif kind == "route":
                    b = step[1]
                    turn = g_turn[step]
                    if b == 0:
                        dve.wait_ge(ld_moe, 16 * 4)
                    wait_g_full(dve, turn)
                    bank = g_bank(turn)[:, 0:QT * E].rearrange("p (q e) -> p q e", q=QT)
                    nc.vector.tensor_tensor(logit[:], bank, bs[:].unsqueeze(1).broadcast_to([128, QT, E]),
                                            ALU.add).then_inc(g_read[turn % 2], 1)
                    wait_g_read(dve, turn)
                    for q in range(QT):
                        last = nc.vector.max(top[:, q, :], logit[:, q, :])
                    link(last)
                    for q in range(QT):
                        last = nc.vector.max_index(top_i[:, q, :], top[:, q, :], logit[:, q, :])
                    link(last)
                    nc.vector.tensor_tensor(dl[:, 0, :], top[:, :, 1], top[:, :, 0], ALU.subtract)\
                        .then_inc(gap_done, 1)
                    link(nc.vector.tensor_copy(top_f[:], top_i[:, :, 0:2]))
                    dve.wait_ge(e_gap, b + 1)
                    link(nc.vector.tensor_scalar(dl[:, 2, :], dl[:, 1, :], 1.0, None, ALU.add))
                    link(nc.vector.reciprocal(tw[:, 0, :], dl[:, 2, :]))
                    link(nc.vector.tensor_scalar(tw[:, 0, :], tw[:, 0, :], gate[:, 3:4], None, ALU.mult))
                    link(nc.vector.tensor_tensor(tw[:, 1, :], tw[:, 0, :], dl[:, 1, :], ALU.mult))
                    for n in range(2):
                        link(nc.vector.tensor_tensor(pick[:, n, :, :], iota[:].unsqueeze(1).broadcast_to([128, QT, E]),
                                                     top_f[:, :, n:n + 1].broadcast_to([128, QT, E]), ALU.is_equal))
                        link(nc.vector.tensor_tensor(pick[:, n, :, :], pick[:, n, :, :],
                                                     tw[:, n, :].unsqueeze(2).broadcast_to([128, QT, E]), ALU.mult))
                    nc.vector.tensor_tensor(comb[:, b, :, :], pick[:, 0, :, :], pick[:, 1, :, :], ALU.add)\
                        .then_inc(routed, 1)
                elif kind == "up":
                    n = step[1]
                    dve.wait_ge(e_silu, n + 1)
                    dve.wait_ge(eu_full, n + 1)
                    if n >= RING:
                        dve.wait_ge(y_added, n - RING + 1)
                    if n == 0:
                        wait_g_full(dve, g_turn[("ffn_down", B - 1)])
                    nc.vector.tensor_tensor(h_all[n % RING], h_silu[n % 2], ps[:, E_BANK[n % 2], :], ALU.mult)\
                        .then_inc(e_hid, 1)
                    if n == B * ET - 1:
                        m = B * E - 1
                        dve.wait_ge(e_hid, n + 1)
                        dve.wait_ge(comb_in[m % RING], 16 * (m // RING + 1))
                        nc.vector.tensor_tensor(h_all[n % RING], h_all[n % RING], comb_row[:, m % RING, :], ALU.mult)\
                            .then_inc(last_weighed, 1)
                elif kind == "weigh":
                    n = step[1]
                    dve.wait_ge(h_hi_done, n + 1)
                    nc.vector.tensor_tensor(h_lo[n % RING], h_all[n % RING], h_hi[n % RING].bitcast(F32),
                                            ALU.subtract).then_inc(h_lo_done, 1)
                elif kind == "finish":
                    b = step[1]
                    dve.wait_ge(tr_full, tr_turn[step] + 1)
                    xb = x[:, b * QT:(b + 1) * QT, :].rearrange("p q d -> p (q d)")
                    nc.vector.tensor_tensor(xb, xb, tr, ALU.add).then_inc(tr_read, 1)

        @block.tensor
        def _(pe):
            def mm(o, lhsT, rhs, start=True, stop=True):
                return nc.tensor.matmul(o, lhsT, rhs, start=start, stop=stop, skip_group_check=True)

            for step in ordered(TIMED, "tensor"):
                kind = step[0]
                if kind == "keys":
                    turn = g_turn[step]
                    if step[1] == 0:
                        pe.wait_ge(ctx_padded, 1)
                        pe.wait_ge(ld_ctx, 32)
                    wait_g_free(pe, turn)
                    mm(g_bank(turn)[:, 0:KW], wk[:, step[1], :], ctx_t[:].rearrange("c b s -> c (b s)"))\
                        .then_inc(g_full[turn % 2], 1)
                elif kind == "values_in":
                    b = step[1]
                    turn = g_turn[step]
                    pe.wait_ge(ctx_ready, 1)
                    pe.wait_ge(ld_v, 16)
                    wait_g_free(pe, turn)
                    bank = g_bank(turn)
                    mm(bank[:, 0:2 * D], ctx_t[:, b, 0:SM], wv[:].rearrange("c l d -> c (l d)"))
                    mm(bank[:, 2 * D:4 * D], ctx_r[:, b, :, :].rearrange("c g k -> c (g k)"),
                       wv[:].rearrange("c l d -> c (l d)")).then_inc(g_full[turn % 2], 1)
                elif kind == "turn":
                    _, i, b = step
                    turn = tr_turn[step]
                    if turn == 0:
                        pe.wait_ge(ld_ident, 16)
                    if turn:
                        pe.wait_ge(tr_read, turn)
                    for q in range(QT):
                        pe.wait_ge(xn_done, QT * normed_no[("normed", i, b)] + q + 1)
                        last = nc.tensor.transpose(tr[:, q * 128:(q + 1) * 128], xn[:, b, q, :], ident[:])
                    last.then_inc(tr_full, 1)
                elif kind == "query":
                    _, l, b = step
                    turn = g_turn[step]
                    wait_g_free(pe, turn)
                    pe.wait_ge(q_scaled, 1)
                    pe.wait_ge(tr_read, tr_turn[("turn", 2 * l, b)] + 1)
                    mm(g_bank(turn), wq[:, l, :], xt[:, b, :]).then_inc(g_full[turn % 2], 1)
                elif kind == "scan":
                    _, u, k = step
                    l, b, j = UNITS[u]
                    n = 2 * QT * u + k
                    if k == 0 and j == 0:
                        pe.wait_ge(q_in[l * B + b], 16 * 3)
                        pe.wait_ge(zeroed, 1 + 2 * l)
                    if k == 0 and b == 0:
                        pe.wait_ge(k_ready[l], j + 1)
                    if n >= 2:
                        pe.wait_ge(a_read, n - 1)
                    half = k % 2
                    queries = q_st[l][:, b, j, (k // 2) * 128:(k // 2 + 1) * 128]
                    o = ps[:, A_BANK[n % 2], 0:2 * S].rearrange("p (h s) -> p h s", h=2)
                    rest = k_st[l][:, j, b, SM * G + 64 * half:SM * G + 64 * (half + 1)]
                    mm(o[:, :, 0:SM], queries, k_st[l][:, j, b, 2 * SM * half:2 * SM * (half + 1)])
                    mm(o[:, :, SM:S], queries, rest.rearrange("p (h s) -> p h s", h=2)[:, :, 0:SR])\
                        .then_inc(a_full, 1)
                elif kind == "shift":
                    u = step[1]
                    turn = tr_turn[step]
                    pe.wait_ge(max_split, u + 1)
                    if turn:
                        pe.wait_ge(tr_read, turn)
                    for q in range(QT):
                        last = nc.tensor.transpose(tr[0:2 * G, q * 128:(q + 1) * 128],
                                                   mx_parts[:, u % 2, q, :, :].rearrange("p a g -> p (a g)"), ident[:])
                    last.then_inc(tr_full, 1)
                elif kind == "exps":
                    _, u, t = step
                    l, b, j = UNITS[u]
                    n = 5 * u + t
                    if t == 0:
                        pe.wait_ge(tr_read, tr_turn[("shift", u)] + 1)
                    if n >= 2:
                        pe.wait_ge(e_read, n - 1)
                    first = SM * G if t == 0 else SM * (t - 1)
                    keys = k_st[l][:, j, b, first:first + SM]
                    mm(ps[:, E_BANK[n % 2], :], keys, q_st[l][:, b, j, :]).then_inc(e_full, 1)
                elif kind == "rests":
                    u = step[1]
                    l, b, j = UNITS[u]
                    if l == 0 and j == 0:
                        wait_g_read(pe, g_turn[("values_in", b)])
                    if l:
                        pe.wait_ge(clamped, 3 * (u - B * J) + 1)
                    else:
                        pe.wait_ge(e_read, 5 * u + 1)
                    if u:
                        pe.wait_ge(pv_read, u)
                    mm(ps[:, PV_BANK, :], v_rest[:, l, b, j, :], ex[:, u % 2, 0, :], stop=False)
                elif kind == "values":
                    u = step[1]
                    l, b, j = UNITS[u]
                    if l:
                        pe.wait_ge(clamped, 3 * (u - B * J + 1))
                    else:
                        pe.wait_ge(e_read, 5 * (u + 1))
                    for g in range(G):
                        last = mm(ps[32 * g:32 * g + DH + 1, PV_BANK, :], v_main[:, l, b, J * g + j, :],
                                  ex[:, u % 2, 1 + g, :], start=False)
                    last.then_inc(pv_full, 1)
                elif kind == "share":
                    u = step[1]
                    turn = tr_turn[step]
                    pe.wait_ge(pv_read, u + 1)
                    pe.wait_ge(tr_read, turn)
                    for q in range(QT):
                        last = nc.tensor.transpose(tr[:, q * 128:(q + 1) * 128], pv[:, u % 2, q * 128:(q + 1) * 128],
                                                   ident[:])
                    last.then_inc(tr_full, 1)
                elif kind == "join":
                    _, l, b = step
                    turn = tr_turn[step]
                    pe.wait_ge(tr_read, turn)
                    pe.wait_ge(tr_read, tr_turn[("share", UNITS.index((l, b, J - 1)))] + 1)
                    for q in range(QT):
                        last = nc.tensor.transpose(tr[:, q * 128:(q + 1) * 128], o_tok[:, b, q, :], ident[:])
                    last.then_inc(tr_full, 1)
                elif kind == "mlp_up":
                    _, b, f = step
                    turn = g_turn[step]
                    if f == 0:
                        pe.wait_ge(ld_mlp, 48)
                        pe.wait_ge(tr_read, tr_turn[("join", 0, b)] + 1)
                    wait_g_free(pe, turn)
                    mm(g_bank(turn), w1[:, f * 128:(f + 1) * 128], o_t[:]).then_inc(g_full[turn % 2], 1)
                elif kind == "mlp_down":
                    b = step[1]
                    turn = g_turn[step]
                    for f in range(2):
                        wait_g_read(pe, g_turn[("mlp_up", b, f)])
                    wait_g_free(pe, turn)
                    for q in range(QT):
                        for f in range(2):
                            last = mm(g_bank(turn)[:, q * D:(q + 1) * D], hid[:, f, q * 128:(q + 1) * 128],
                                      w2[:, f, :], start=(f == 0), stop=(f == 1))
                    last.then_inc(g_full[turn % 2], 1)
                elif kind == "out_proj":
                    b = step[1]
                    turn = g_turn[step]
                    pe.wait_ge(ld_moe, 16 * 4)
                    pe.wait_ge(tr_read, tr_turn[("join", 1, b)] + 1)
                    wait_g_free(pe, turn)
                    for q in range(QT):
                        last = mm(g_bank(turn)[:, q * D:(q + 1) * D], o_t[:, q * 128:(q + 1) * 128], wo[:])
                    last.then_inc(g_full[turn % 2], 1)
                elif kind == "ffn_up":
                    _, b, f = step
                    turn = g_turn[step]
                    if f == 0:
                        pe.wait_ge(f_ready, 1)
                        pe.wait_ge(tr_read, tr_turn[("turn", 1, b)] + 1)
                    for n in range(2):
                        wait_g_free(pe, turn + n)
                        mm(g_bank(turn + n), f_w[:, n, f * 128:(f + 1) * 128], xt[:, b, :])\
                            .then_inc(g_full[(turn + n) % 2], 1)
                elif kind == "ffn_down":
                    b = step[1]
                    turn = g_turn[step]
                    for f in range(3):
                        wait_g_read(pe, g_turn[("ffn_up", b, f)] + 1)
                    wait_g_free(pe, turn)
                    for q in range(QT):
                        for f in range(3):
                            last = mm(g_bank(turn)[:, q * D:(q + 1) * D], hid[:, f, q * 128:(q + 1) * 128],
                                      f_w[:, 2, f * 128:(f + 1) * 128], start=(f == 0), stop=(f == 2))
                    last.then_inc(g_full[turn % 2], 1)
                elif kind == "route":
                    b = step[1]
                    turn = g_turn[step]
                    pe.wait_ge(tr_read, tr_turn[("turn", 3, b)] + 1)
                    wait_g_free(pe, turn)
                    for q in range(QT):
                        last = mm(g_bank(turn)[:, q * E:(q + 1) * E], xt[:, b, q * 128:(q + 1) * 128], ws[:])
                    last.then_inc(g_full[turn % 2], 1)
                elif kind == "comb":
                    b = step[1]
                    turn = tr_turn[step]
                    pe.wait_ge(routed, b + 1)
                    pe.wait_ge(tr_read, turn)
                    for q in range(QT):
                        last = nc.tensor.transpose(tr[0:E, q * 128:(q + 1) * 128], comb[:, b, q, :], ident[:])
                    last.then_inc(tr_full, 1)
                elif kind == "up":
                    n = step[1]
                    b, t = n // ET, n % ET
                    if t == 0:
                        pe.wait_ge(halves_done, b + 1)
                    if n == 0:
                        pe.wait_ge(split_lo, 3 * CHUNKS)
                        pe.wait_ge(a_read, 2 * QT * LAST)
                        pe.wait_ge(e_read, 5 * LAST)
                    cols = slice(t * 128, (t + 1) * 128)
                    for w, bank, full, used in ((0, A_BANK, eg_full, e_silu), (1, E_BANK, eu_full, e_hid)):
                        if n >= 2:
                            pe.wait_ge(used, n - 1)
                        o = ps[:, bank[n % 2], :]
                        mm(o, w_hi[w][:, cols], x_hi[:, b, :], stop=False)
                        mm(o, w_hi[w][:, cols], x_lo[:, b, :], start=False, stop=False)
                        mm(o, w_lo(w, cols.start, cols.stop), x_hi[:, b, :], start=False).then_inc(full, 1)
                elif kind == "down":
                    n = step[1]
                    b, t = n // ET, n % ET
                    if n == 0:
                        pe.wait_ge(pv_read, LAST)
                    if n == ET:
                        for turn in (G_TURNS - 2, G_TURNS - 1):
                            wait_g_read(pe, turn)
                    o = ps[:, Y_BANK[b], :]
                    cols = slice(t * 128, (t + 1) * 128)
                    pe.wait_ge(h_hi_done, n + 1)
                    hi, lo = h_hi[n % RING], h_lo[n % RING]
                    mm(o, w_hi[2][:, cols], hi, start=(t == 0), stop=False)
                    mm(o, w_lo(2, cols.start, cols.stop), hi, start=False, stop=False)
                    pe.wait_ge(h_lo_done, n + 1)
                    mm(o, w_hi[2][:, cols], lo, start=False, stop=(t == ET - 1)).then_inc(y_added, 1)
                elif kind == "finish":
                    b = step[1]
                    turn = tr_turn[step]
                    pe.wait_ge(y_read, b + 1)
                    pe.wait_ge(tr_read, turn)
                    for q in range(QT):
                        last = nc.tensor.transpose(tr[:, q * 128:(q + 1) * 128], pv[:, b, q * 128:(q + 1) * 128],
                                                   ident[:])
                    last.then_inc(tr_full, 1)


def kernel(**inputs):
    import numpy as _np
    import concourse.bacc as _bacc
    from concourse import mybir as _mybir
    from concourse.bass_utils import run_bass_kernel_spmd as _run

    i = {k: _np.asarray(v) for k, v in inputs.items()}
    tok = lambda v: v.reshape(B, QT, 128, D).transpose(0, 2, 1, 3)
    heads = lambda v: v.reshape(-1, G, J, DH).transpose(0, 1, 3, 2).reshape(-1, D)
    row = lambda v, n=128: _np.broadcast_to(v.reshape(1, -1), (n, v.size))
    ctx_rows = lambda w, b: _np.concatenate([w, b.reshape(1, -1)], 0)
    head_mask = _np.zeros((128, G), _np.float32)
    for g in range(G):
        for r in range(3):
            head_mask[32 * r + DH * g:32 * r + DH * (g + 1), g] = 1.0
        head_mask[[96 + g, 96 + G + g], g] = -1.0
    is_rest = (_np.arange(128) % 32 < SR).astype(_np.float32).reshape(128, 1)
    order = [hidden_block(t, r) for t in range(ET) for r in range(4)]

    def tiles(w):
        blocks = _np.pad(w, ((0, 0), (0, 0), (0, FP - EF))).reshape(E, D, FP // 32, 32)
        return _np.stack([blocks[e, :, n, :] for e, n in order], 1).reshape(D, ET * 128)

    arrays = {
        "x": tok(i["x"]),
        "ctx_t": i["ctx_768"].transpose(2, 0, 1),
        "wk": _np.stack([ctx_rows(heads(i[f"L{l}_xattn_Wk"]), heads(i[f"L{l}_xattn_bk"])) for l in range(2)], 1),
        "wv": _np.stack([ctx_rows(i[f"L{l}_xattn_Wv"], i[f"L{l}_xattn_bv"]) for l in range(2)], 1),
        "wq": _np.stack([heads(i[f"L{l}_xattn_Wq"]) for l in range(2)], 1),
        "bq": _np.stack([heads(i[f"L{l}_xattn_bq"])[0] for l in range(2)], 1),
        "is_rest": is_rest,
        "head_mask": head_mask,
        "ident": _np.eye(128, dtype=_np.float32),
        "iota": row(_np.arange(E, dtype=_np.float32)),
        "gates": row(_np.concatenate([i["g_xattn"], i["g_ffn"]])),
        "bias_out": _np.broadcast_to(_np.stack([i["L0_xattn_b2"], i["L1_xattn_bo"]])[None], (128, 2, D)),
        "w1": i["L0_xattn_W1"], "b1": i["L0_xattn_b1"].reshape(2, 128).T,
        "w2": i["L0_xattn_W2"].reshape(2, 128, D).transpose(1, 0, 2),
        "wo": i["L1_xattn_Wo"],
        "f_int": _np.stack([i["L0_ffn_w_gate"].T, i["L0_ffn_w_up"].T,
                            i["L0_ffn_w_down"].T.reshape(3, 128, D).transpose(1, 0, 2).reshape(128, FH)], 1),
        "ws": i["L1_ffn_Ws"], "bs": row(i["L1_ffn_bs"]),
        "experts": _np.stack([tiles(i["L1_ffn_Wg"]), tiles(i["L1_ffn_Wu"]),
                              tiles(i["L1_ffn_Wd"].transpose(0, 2, 1)).reshape(D, ET, 128)
                              .transpose(2, 1, 0).reshape(128, ET * D)], 1),
    }
    arrays = {k: _np.ascontiguousarray(v) for k, v in arrays.items()}
    nc = _bacc.Bacc("TRN2", target_bir_lowering=False, num_devices=1)
    aps = {k: nc.dram_tensor(f"in_{k}", v.shape, _mybir.dt.from_np(v.dtype), kind="ExternalInput").ap()
           for k, v in arrays.items()}
    out = nc.dram_tensor("out", (B, 128, QT, D), _mybir.dt.float32, kind="ExternalOutput").ap()
    comb_rows = nc.dram_tensor("comb_rows", (B, E, T), _mybir.dt.float32, kind="Internal").ap()
    flamingo(nc, aps, comb_rows, out)
    got = _run(nc, [{f"in_{k}": v for k, v in arrays.items()}], core_ids=[0]).results[0]["out"]
    return _np.asarray(got).reshape(B, 128, QT, D).transpose(0, 2, 1, 3).reshape(B, T, D)
```
